# Optimizing a Trainium2 kernel written in Bass

```python
import numpy as np
import jax
import jax.numpy as jnp

def _softmax(x, axis=-1):
    return jax.nn.softmax(x, axis=axis)

def _gelu(x):
    return jax.nn.gelu(x, approximate=True)

def _silu(x):
    return jax.nn.silu(x)

def _sigmoid(x):
    return jax.nn.sigmoid(x)

def _layernorm(x, axis=-1, eps=1e-05):
    m = jnp.mean(x, axis=axis, keepdims=True)
    v = jnp.var(x, axis=axis, keepdims=True)
    return (x - m) / jnp.sqrt(v + eps)

def _scatter_add(tgt, idx, src, axis=0):
    return tgt.at[idx].add(src)

def _segment_sum(src, seg, n):
    return jax.ops.segment_sum(src, seg, n)
kernel_name = 'mk_gnn_resnorm_d2_gnn_r8_bb72da'

def setup_inputs(seed: int=0):
    np.random.seed(seed)
    _w = jnp.asarray

    def _rec_inputs():
        import jax
        import jax.numpy as jnp
        _gk = jax.random.key(seed)
        x = -0.0003713 + 1 * jax.random.normal(jax.random.fold_in(_gk, 1), (6250, 128), jnp.float32)
        src = jax.random.randint(jax.random.fold_in(_gk, 2), (200000,), 0, 6250, jnp.int32)
        dst = jax.random.randint(jax.random.fold_in(_gk, 3), (200000,), 0, 6250, jnp.int32)
        _o = jnp.argsort(dst, stable=True)
        src = src[_o]
        dst = dst[_o]
        edge_type_32 = jax.random.randint(jax.random.fold_in(_gk, 13), (200000,), 0, 32, jnp.int32)
        edge_weight = jax.random.uniform(jax.random.fold_in(_gk, 14), (200000,), jnp.float32, 0.0, 0.999998)
        edge_weight1 = jax.random.uniform(jax.random.fold_in(_gk, 15), (200000, 1), jnp.float32, 0.0, 0.999998)
        return (x, src, dst, edge_type_32, edge_weight, edge_weight1)
    x, src, dst, edge_type_32, edge_weight, edge_weight1 = _rec_inputs()

    def _L0_gnn_setup():
        import jax, jax.numpy as jnp
        import numpy as np
        EPS_WSUM = 1e-12
        EPS_NORM = 1e-12

        def _weighted_neighbor_mean(x, src, dst, w):
            msgs = x[dst] * w[:, None]
            num_nodes = x.shape[0]
            agg = jax.ops.segment_sum(msgs, src, num_segments=num_nodes)
            wsum = jax.ops.segment_sum(w, src, num_segments=num_nodes)
            return agg / jnp.maximum(wsum, EPS_WSUM)[:, None]

        def _sage_layer(x, src, dst, w, W, b):
            neigh = _weighted_neighbor_mean(x, src, dst, w)
            h = jnp.concatenate([x, neigh], axis=1)
            h = h @ W.T + b
            return jax.nn.relu(h)
        key = jax.random.key(seed)
        ks = jax.random.split(key, 8)
        N, E, D = (12500, 100000, 128)
        x = jax.random.normal(ks[0], (N, D), dtype=jnp.float32)
        edge_index = jax.random.randint(ks[1], (2, E), 0, N, dtype=jnp.int64)
        edge_weight = jax.random.uniform(ks[2], (E,), dtype=jnp.float32)
        W1 = jax.random.normal(ks[3], (D, 2 * D), dtype=jnp.float32) * (1.0 / np.sqrt(2 * D))
        b1 = jnp.zeros((D,), dtype=jnp.float32)
        W2 = jax.random.normal(ks[4], (D, 2 * D), dtype=jnp.float32) * (1.0 / np.sqrt(2 * D))
        b2 = jnp.zeros((D,), dtype=jnp.float32)
        return {'x': x, 'edge_index': edge_index, 'edge_weight': edge_weight, 'W1': W1, 'b1': b1, 'W2': W2, 'b2': b2}
    _L0_gnn_all = _L0_gnn_setup()
    _L0_gnn_in = {k: v for k, v in _L0_gnn_all.items() if k in ('W1', 'b1', 'W2', 'b2')}
    del _L0_gnn_all

    def _L1_gnn_setup():
        import jax, jax.numpy as jnp
        import numpy as np
        N_NODES = 6250
        N_EDGES = 62500
        IN_FEAT = 128
        OUT_FEAT = 128
        NUM_RELS = 32
        NUM_BASES = 8
        key = jax.random.key(seed)
        ks = jax.random.split(key, 8)
        h = jax.random.normal(ks[0], (N_NODES, IN_FEAT), dtype=jnp.float32)
        src = jax.random.randint(ks[1], (N_EDGES,), 0, N_NODES, dtype=jnp.int32)
        dst = jax.random.randint(ks[2], (N_EDGES,), 0, N_NODES, dtype=jnp.int32)
        etype = jax.random.randint(ks[3], (N_EDGES,), 0, NUM_RELS, dtype=jnp.int32)
        norm = jax.random.uniform(ks[4], (N_EDGES, 1), dtype=jnp.float32)
        weight = jax.random.normal(ks[5], (NUM_BASES, IN_FEAT, OUT_FEAT), dtype=jnp.float32) * 0.05
        w_comp = jax.random.normal(ks[6], (NUM_RELS, NUM_BASES), dtype=jnp.float32) * 0.3
        bias_param = jax.random.normal(ks[7], (OUT_FEAT,), dtype=jnp.float32) * 0.05
        return {'h': h, 'src': src, 'dst': dst, 'etype': etype, 'norm': norm, 'weight': weight, 'w_comp': w_comp, 'bias_param': bias_param}
    _L1_gnn_all = _L1_gnn_setup()
    _L1_gnn_in = {k: v for k, v in _L1_gnn_all.items() if k in ('weight', 'w_comp', 'bias_param')}
    del _L1_gnn_all
    return {'x': x, 'src': src, 'dst': dst, 'edge_type_32': edge_type_32, 'edge_weight': edge_weight, 'edge_weight1': edge_weight1, 'L0_gnn_W1': _L0_gnn_in['W1'], 'L0_gnn_b1': _L0_gnn_in['b1'], 'L0_gnn_W2': _L0_gnn_in['W2'], 'L0_gnn_b2': _L0_gnn_in['b2'], 'L1_gnn_weight': _L1_gnn_in['weight'], 'L1_gnn_w_comp': _L1_gnn_in['w_comp'], 'L1_gnn_bias_param': _L1_gnn_in['bias_param']}

def reference(x, src, dst, edge_type_32, edge_weight, edge_weight1, L0_gnn_W1, L0_gnn_b1, L0_gnn_W2, L0_gnn_b2, L1_gnn_weight, L1_gnn_w_comp, L1_gnn_bias_param):
    import jax
    import jax.numpy as jnp

    def _L0_gnn_ref(x, edge_index, edge_weight, W1, b1, W2, b2):
        import jax, jax.numpy as jnp
        import numpy as np
        EPS_WSUM = 1e-12
        EPS_NORM = 1e-12

        def _weighted_neighbor_mean(x, src, dst, w):
            msgs = x[dst] * w[:, None]
            num_nodes = x.shape[0]
            agg = jax.ops.segment_sum(msgs, src, num_segments=num_nodes)
            wsum = jax.ops.segment_sum(w, src, num_segments=num_nodes)
            return agg / jnp.maximum(wsum, EPS_WSUM)[:, None]

        def _sage_layer(x, src, dst, w, W, b):
            neigh = _weighted_neighbor_mean(x, src, dst, w)
            h = jnp.concatenate([x, neigh], axis=1)
            h = h @ W.T + b
            return jax.nn.relu(h)
        src = edge_index[0]
        dst = edge_index[1]
        h = _sage_layer(x, src, dst, edge_weight, W1, b1)
        h = _sage_layer(h, src, dst, edge_weight, W2, b2)
        norm = jnp.linalg.norm(h, axis=1, keepdims=True)
        return h / jnp.maximum(norm, EPS_NORM)

    def _L1_gnn_ref(h, src, dst, etype, norm, weight, w_comp, bias_param):
        import jax, jax.numpy as jnp
        import numpy as np
        N_NODES = 6250
        N_EDGES = 62500
        IN_FEAT = 128
        OUT_FEAT = 128
        NUM_RELS = 32
        NUM_BASES = 8
        hsrc = h[src]
        coef = w_comp[etype]
        msg = jnp.zeros((hsrc.shape[0], weight.shape[2]), dtype=h.dtype)
        for b in range(weight.shape[0]):
            msg = msg + hsrc @ weight[b] * coef[:, b][:, None]
        msg = msg * norm
        node_repr = jax.ops.segment_sum(msg, dst, num_segments=h.shape[0])
        node_repr = node_repr + bias_param
        return jax.nn.relu(node_repr)
    edge_index = jnp.stack([src, dst])
    x = _layernorm(x + _L0_gnn_ref(x, edge_index, edge_weight, L0_gnn_W1, L0_gnn_b1, L0_gnn_W2, L0_gnn_b2), axis=-1)
    x = _layernorm(x + _L1_gnn_ref(x, src, dst, edge_type_32, edge_weight1, L1_gnn_weight, L1_gnn_w_comp, L1_gnn_bias_param), axis=-1)
    return x

_drawn_inputs = setup_inputs


def setup_inputs(seed=0):
    import zlib

    import numpy as np

    out = dict(_drawn_inputs(seed))
    spreads = {'L0_gnn_b1': (0.0, 0.565), 'L0_gnn_b2': (0.0, 0.343)}
    factors = {'edge_weight': 5.58}
    for name, (base, spread) in spreads.items():
        noise = np.random.default_rng([zlib.crc32(name.encode()), seed]).standard_normal(out[name].shape)
        drawn = base * np.exp(spread * noise) if base else spread * noise
        out[name] = jnp.asarray(drawn.astype(out[name].dtype))
    for name, factor in factors.items():
        out[name] = (out[name] * factor).astype(out[name].dtype)
    return out
```

```python
import numpy as np
import concourse.bass as bass
from concourse import mybir
from contextlib import ExitStack

P = 128
N, E, D = 6250, 200000, 128
RELS, BASES = 32, 8
NBLK = -(-N // P)
NPAD = NBLK * P
NFULL = N // P
NREST = N - NFULL * P
SEPT = 7
NSEPT = NBLK // SEPT
COLS = 1568
LAST = E - (P - 1) * COLS
RING = 16
HALF, QUART = 8, 4
EPS_WSUM, EPS_NORM, EPS_LN = 1e-12, 1e-12, 1e-5
TRASH = float(1 << 25)

F32, I32, BF16 = mybir.dt.float32, mybir.dt.int32, mybir.dt.bfloat16
ALU = mybir.AluOpType
ACT = mybir.ActivationFunctionType
AX = mybir.AxisListType.X


def up(n, m):
    return -(-n // m) * m


def due(count):
    return not (isinstance(count, int) and count == 0)


def rounds(eng, n, step):
    step(0)
    with eng.Fori(1, n) as i:
        step(i)


def rounds_ahead(eng, n, step):
    step(0, True)
    with eng.Fori(1, n - 1) as i:
        step(i, True)
    step(n - 1, False)


class Sort:

    def __init__(self, shift, lanes):
        self.shift, self.window = shift, 1 << shift
        self.bins = NPAD >> shift
        self.wide = self.bins + 1
        self.lanes = lanes
        self.cells = lanes * self.wide
        self.groups = COLS // lanes
        self.per_half = HALF // lanes
        self.tiles = up((E + self.bins * (P - 1)) // P, RING)
        self.chunks = up(self.bins, P) // P


SORTS = [Sort(7, 8), Sort(5, 2)]
W1 = SORTS[1].window
LSORT = [0, 0, 1]
ROUNDS = [SORTS[s].tiles // RING for s in LSORT]
R0 = [0, ROUNDS[0], ROUNDS[0] + ROUNDS[1], sum(ROUNDS)]
T0 = [QUART * r for r in R0]


def build(nc, x, src, dst, etype, w, w1, W1m, b1, W2m, b2, Wrel, wcomp, brel, out):
    with ExitStack() as ctx:
        def sb(name, shape, dt=F32):
            return ctx.enter_context(nc.sbuf_tensor(name, shape, dt))

        def sem(name):
            return ctx.enter_context(nc.semaphore(name))

        rec_d = [nc.dram_tensor(f"rec{s}", [P * SORTS[s].tiles, 4], I32).ap() for s in range(2)]
        h1_d = nc.dram_tensor("h1_table", [NPAD, D], F32).ap()
        x1_d = nc.dram_tensor("x1_table", [NPAD, D], F32).ap()

        raw = sb("raw", [P, 5, COLS], I32)
        SRC, DST, ET, WT, WT1 = range(5)
        rawf = raw[:].bitcast(F32)
        S = [sb(f"S{s}", [P, SORTS[s].tiles, 4], I32) for s in range(2)]
        Sf = [t[:].bitcast(F32) for t in S]
        X = sb("X", [P, NBLK, D])
        H1 = sb("H1", [P, NBLK, D])
        big = sb("big", [P, NBLK * (D + 1)])
        agg = big[:].rearrange("p (b c) -> p b c", c=D + 1)
        reprT = big[:, 0:NPAD]
        G = sb("G", [P, RING, D + 1])
        sel = sb("sel", [P, RING, P])
        ident = sb("ident", [P, P])
        strict = sb("strict", [P, P], BF16)
        comp = sb("comp", [P, P], BF16)
        ones = sb("ones", [P, P], BF16)
        onesf = sb("onesf", [1, P])
        iota_i = sb("iota_i", [P, 256], I32)
        iota_b = sb("iota_b", [P, 256], BF16)
        iota_f = sb("iota_f", [P, P])
        oh = sb("oh", [P, 2, 400], BF16)
        prod = sb("prod", [P, 400])
        start = sb("start", [P, 400])
        tot = sb("tot", [P, 4, 200])
        toti = sb("toti", [P, 200], I32)
        col = sb("col", [P, 2])
        table = sb("table", [33, SORTS[1].tiles], I32)
        posi = sb("posi", [P, 3, HALF], I32)
        idx = sb("idx", [P, RING], I32)
        rring = sb("rring", [P, RING, 4], I32)
        rringf = rring[:].bitcast(F32)
        small = sb("small", [P, 8, SEPT])
        WT_sb = sb("WT_sb", [P, 4, D])
        bias = sb("bias", [1, 2, D])
        Wr = sb("Wr", [P, BASES, D])
        wcd = sb("wcd", [P, QUART, BASES])
        brel_c = sb("brel_c", [P, 1])

        early = H1[:].rearrange("p a b -> p (a b)")
        wtmp = H1[:, 0:4, :]
        kt = early[:, 512:512 + COLS].bitcast(I32)
        kl = early[:, 2112:2112 + COLS].bitcast(I32)
        tiota = early[:, 3712:3712 + SORTS[1].tiles]
        mark = [big[:, 1024 * j:1024 * j + 1024].bitcast(BF16) for j in range(2)]
        keys = big[:, 2048:2048 + COLS + HALF].bitcast(BF16).rearrange("p (s c) -> p s c", s=2)
        locs = big[:, 3648:3648 + COLS].bitcast(BF16).rearrange("p (s c) -> p s c", s=2)
        flat = rawf.rearrange("p a c -> p (a c)")

        def stage(a, n):
            return flat[:, a * SEPT * D:(a + n) * SEPT * D]

        xst = stage(0, 1)
        nst = stage(1, 1)
        xnT = stage(2, 2)
        y = stage(4, 1).rearrange("p (b c) -> p b c", c=D)
        sq = stage(5, 1).rearrange("p (b c) -> p b c", c=D)
        C = H1[:, 0:32, :].rearrange("p a b -> p (a b)").rearrange("p (t b j) -> p t b j", b=BASES, j=W1)
        Ub = Sf[0][:, 0:1024, :].rearrange("p t w -> p (t w)").rearrange("p (b t j) -> p b t j", t=RING, j=W1)
        rel = sel[:, 0:4, :].rearrange("p a b -> p (a b)").rearrange("p (t j) -> p t j", j=RELS)
        place = sel[:, 4:8, :].rearrange("p a b -> p (a b)").rearrange("p (t j) -> p t j", j=W1)
        relT = sel[:, 8:12, :]
        cn = sel[:, 12, :].rearrange("p (t b) -> p t b", b=BASES)

        PS = ctx.enter_context(nc.psum_tensor("PS", [P, 8 * 512], F32))

        def bank(b, n=512, off=0):
            return PS[:, b * 512 + off:b * 512 + off + n]

        def sums(t):
            return bank(t // 2, D + 1, (t % 2) * 256)

        s_tail = sem("tail_preset")
        s_preset = sem("areas_preset")
        s_edges = sem("edges_loaded")
        s_nodes = sem("nodes_loaded")
        s_small = sem("weights_loaded")
        s_go = sem("pool_go")
        s_iota = sem("iota_made")
        s_filled = sem("masks_filled")
        s_const = sem("masks_made")
        s_ones = sem("ones_made")
        s_zeroed = sem("records_zeroed")
        s_dve = sem("dve_chain")
        s_wt = sem("weights_transposed")
        s_wtc = sem("weights_copied")
        s_out = sem("out_stored")
        srt = []
        for s in range(2):
            names = ["keys", "blank", "opened", "count_oh", "counted", "start", "marks", "marked",
                     "oh", "ranked", "prod", "summed", "pos", "split", "idx", "rec", "loaded"]
            d = {n: sem(f"sort{s}_{n}") for n in names}
            d["scat"] = [sem(f"sort{s}_scat{h}") for h in range(2)]
            srt.append(d)
        shared = {n: [sem(f"ring_{n}{q}") for q in range(4)] for n in ("idx", "rec", "sel", "mm", "add")}
        lay = []
        for l in range(3):
            names = ["xst", "nst", "tr", "trc", "lin", "relu", "nchain", "for_root", "root",
                     "stored", "stored_dma"]
            if l == 2:
                names += ["rel", "relT", "relTc", "coef", "node", "coefn", "cmat", "w", "uc"]
            d = {n: sem(f"layer{l}_{n}") for n in names}
            d["gath"] = [sem(f"layer{l}_gath{q}") for q in range(4)]
            for n in shared:
                d[n] = shared[n]
            lay.append(d)

        N_EDGES, N_NODES, N_SMALL = 16 * 15, 32, 16 * (5 + QUART + 1)
        block = ctx.enter_context(nc.Block())

        def rows(t, b0, nb):
            return t[b0 * P:(b0 + nb) * P, :].rearrange("(b p) c -> p b c", p=P)

        def scattered(eng, s):
            for h in range(2):
                eng.wait_ge(srt[s]["scat"][h], COLS // 2 * 16)

        @block.sync
        def _(sp):
            sp.wait_ge(s_tail, 2)
            for a, t in ((SRC, src), (WT, w), (DST, dst), (ET, etype), (WT1, w1)):
                view = raw[:] if a <= ET else rawf
                for p0, p1 in ((0, 112), (112, 127)):
                    sp.dma_start(view[p0:p1, a, :], t[p0 * COLS:p1 * COLS].rearrange("(p c) -> p c", c=COLS)).then_inc(s_edges, 16)
                sp.dma_start(view[127:128, a, 0:LAST], t[127 * COLS:E].rearrange("(p c) -> p c", p=1)).then_inc(s_edges, 16)
            sp.wait_ge(s_preset, 6)
            for s in range(2):
                sp.dma_start(rec_d[s].rearrange("(p t) c -> p (t c)", p=P), S[s][:].rearrange("p t c -> p (t c)")).then_inc(s_zeroed, 16)
            sp.dma_start(X[:, 0:NFULL, :], rows(x, 0, NFULL)).then_inc(s_nodes, 16)
            sp.dma_start(X[0:NREST, NFULL, :], x[NFULL * P:N, :]).then_inc(s_nodes, 16)
            sp.dma_start(H1[:, 0:2, :], W1m.rearrange("o (h i) -> o h i", h=2)).then_inc(s_small, 16)
            sp.dma_start(H1[:, 2:4, :], W2m.rearrange("o (h i) -> o h i", h=2)).then_inc(s_small, 16)
            sp.dma_start(bias[:, 0, :], b1.rearrange("(a c) -> a c", a=1)).then_inc(s_small, 16)
            sp.dma_start(bias[:, 1, :], b2.rearrange("(a c) -> a c", a=1)).then_inc(s_small, 16)
            sp.dma_start(Wr[:], Wrel.rearrange("b i o -> i b o")).then_inc(s_small, 16)
            for k in range(QUART):
                sp.dma_start(wcd[k * RELS:(k + 1) * RELS, k, :], wcomp).then_inc(s_small, 16)
            with nc.allow_non_contiguous_dma(reason="128 words, once"):
                sp.dma_start(brel_c[:], brel.rearrange("(p a) -> p a", a=1)).then_inc(s_small, 16)
            for s in range(2):
                scattered(sp, s)
                sp.dma_start(S[s][:].rearrange("p t c -> p (t c)"), rec_d[s].rearrange("(p t) c -> p (t c)", p=P)).then_inc(srt[s]["loaded"], 16)
            for l, (t, table_d) in enumerate(((H1, h1_d), (X, x1_d))):
                for i in range(NSEPT):
                    sp.wait_ge(lay[l]["stored"], i + 1)
                    sp.dma_start(rows(table_d, i * SEPT, SEPT), t[:, i * SEPT:(i + 1) * SEPT, :]).then_inc(lay[l]["stored_dma"], 16)
            for i in range(NSEPT):
                sp.wait_ge(lay[2]["stored"], i + 1)
                n = min(SEPT, NFULL - i * SEPT)
                sp.dma_start(rows(out, i * SEPT, n), X[:, i * SEPT:i * SEPT + n, :]).then_inc(s_out, 16)
            sp.dma_start(out[NFULL * P:N, :], X[0:NREST, NFULL, :]).then_inc(s_out, 16)
            sp.wait_ge(s_out, 16 * (NSEPT + 1))

        @block.gpsimd
        def _(pool):
            nc.gpsimd.memset(raw[:, 0:2, LAST:], NPAD).then_inc(s_tail, 1)
            nc.gpsimd.memset(raw[:, 2:5, LAST:], 0).then_inc(s_tail, 1)
            nc.gpsimd.iota(iota_i[:], [[1, 256]], base=0, channel_multiplier=0).then_inc(s_iota, 1)
            for m in (strict, comp, ident):
                nc.gpsimd.memset(m[:], 1.0).then_inc(s_filled, 1)
            pool.wait_ge(s_filled, 3)
            for m, op, sign in ((strict, ALU.is_gt, 1), (comp, ALU.is_ge, -1), (ident, ALU.is_equal, 1)):
                nc.gpsimd.affine_select(out=m[:], in_=m[:], compare_op=op, fill=0.0, base=0,
                                        pattern=[[sign, P]], channel_multiplier=-sign).then_inc(s_const, 1)
            nc.gpsimd.iota(tiota, [[1, SORTS[1].tiles]], base=0, channel_multiplier=0,
                           allow_small_or_imprecise_dtypes=True).then_inc(s_iota, 1)
            for s in range(2):
                nc.gpsimd.memset(S[s][:], 0).then_inc(s_preset, 1)
            nc.gpsimd.memset(X[:, NFULL, :], 0.0).then_inc(s_preset, 1)
            nc.gpsimd.memset(wcd[:], 0.0).then_inc(s_preset, 1)
            nc.gpsimd.memset(G[:, :, D:D + 1], 1.0).then_inc(s_preset, 1)
            nc.gpsimd.memset(small[:], 0.0).then_inc(s_preset, 1)
            pool.wait_ge(s_zeroed, 32)
            for s, st in enumerate(SORTS):
                d = srt[s]
                def step(i):
                    for h in range(2):
                        pool.wait_ge(d["rec"], i * 8 + h * 4 + 4)
                        pool.wait_ge(d["idx"], i * 2 + h + 1)
                        pool.sem_inc(s_go, 1)
                        for k in range(h * HALF, (h + 1) * HALF):
                            pool.indirect_dma_start(
                                rec_d[s], bass.IndirectOffsetOnAxis(ap=idx[:, k:k + 1], axis=0),
                                rring[:, k, :], None, bounds_check=P * st.tiles - 1,
                                oob_is_err=False).then_inc(d["scat"][h], 16)

                rounds(pool, COLS // RING, step)
            for l, tab in enumerate((x, h1_d, x1_d)):
                d = lay[l]
                if l:
                    pool.wait_ge(lay[l - 1]["stored_dma"], 16 * NSEPT)
                def step(i):
                    for q in range(4):
                        if due(i * QUART + T0[l]):
                            pool.wait_ge(d["mm"][q], i * QUART + T0[l])
                        pool.wait_ge(d["idx"][q], i + (1 + R0[l]))
                        pool.sem_inc(s_go, 1)
                        for k in range(q * QUART, (q + 1) * QUART):
                            pool.indirect_dma_start(
                                G[:, k, 0:D], None, tab,
                                bass.IndirectOffsetOnAxis(ap=idx[:, k:k + 1], axis=0)).then_inc(d["gath"][q], 16)

                rounds(pool, SORTS[LSORT[l]].tiles // RING, step)

        @block.scalar
        def _(act):
            for s in range(2):
                d = srt[s]
                act.wait_ge(d["keys"], 1)
                if s:
                    scattered(act, 0)
                words = ((raw[:, DST, :], locs[:, 0, :], rawf[:, WT, :], locs[:, 0, :]),
                         (raw[:, SRC, :], locs[:, 1, :], rawf[:, WT1, :], raw[:, ET, :]))[s]
                def step(i):
                    for h in range(2):
                        if due(i * (HALF * 16)):
                            act.wait_ge(d["scat"][h], i * (HALF * 16))
                        for wd, a in enumerate(words):
                            to = (rringf if wd else rring)[:, h * HALF:(h + 1) * HALF, wd]
                            nc.scalar.activation(to, a[:, bass.ds(i * RING + h * HALF, HALF)], ACT.Copy).then_inc(d["rec"], 1)

                rounds(act, COLS // RING, step)
            act.wait_ge(s_nodes, N_NODES)
            act.wait_ge(s_wt, 1)
            nc.scalar.activation(WT_sb[:].rearrange("p a b -> p (a b)"), bank(7), ACT.Copy).then_inc(s_wtc, 1)
            scattered(act, 1)
            for l in range(2):
                d = lay[l]
                if l == 0:
                    act.wait_ge(srt[0]["loaded"], 16)
                else:
                    for q in range(4):
                        act.wait_ge(lay[0]["gath"][q], SORTS[0].tiles // 4 * 16)
                        act.wait_ge(lay[0]["sel"][q], T0[1])
                def step(i):
                    for q in range(4):
                        ks = slice(q * QUART, (q + 1) * QUART)
                        frm = bass.ds(i * RING + q * QUART, QUART)
                        if due(i * (QUART * 16)):
                            act.wait_ge(d["gath"][q], i * (QUART * 16))
                        nc.scalar.activation(idx[:, ks], S[0][:, frm, 0], ACT.Copy).then_inc(d["idx"][q], 1)
                        if due(i * QUART + T0[l]):
                            act.wait_ge(d["sel"][q], i * QUART + T0[l])
                        nc.scalar.activation(rringf[:, ks, 1:3], Sf[0][:, frm, 1:3], ACT.Copy).then_inc(d["rec"][q], 1)

                rounds(act, SORTS[0].tiles // RING, step)
                def step(i):
                    if due(i):
                        act.wait_ge(d["tr"], i)
                    nc.scalar.activation(xst.rearrange("p (b c) -> p b c", c=D), (X, H1)[l][:, bass.ds(i * SEPT, SEPT), :], ACT.Copy).then_inc(d["xst"], 1)
                    if due(i):
                        act.wait_ge(d["lin"], i)
                    act.wait_ge(d["tr"], i + 1)
                    nc.scalar.activation(xnT.rearrange("p (h c) -> p h c", h=2),
                                         PS[:, 0:2048].rearrange("p (h c) -> p h c", h=2)[:, :, 0:SEPT * D], ACT.Copy).then_inc(d["trc"], 1)
                    act.wait_ge(d["lin"], i + 1)
                    if l == 0:
                        nc.scalar.activation(H1[:, bass.ds(i * SEPT, SEPT), :], PS[:, 2048:2048 + SEPT * D].rearrange("p (b c) -> p b c", c=D), ACT.Relu).then_inc(d["stored"], 1)
                    else:
                        if due(i):
                            act.wait_ge(d["stored"], i)
                        nc.scalar.activation(y, PS[:, 2048:2048 + SEPT * D].rearrange("p (b c) -> p b c", c=D), ACT.Relu).then_inc(d["relu"], 1)
                        act.wait_ge(d["for_root"], i * 2 + 1)
                        nc.scalar.activation(small[:, 1, :], small[:, 0, :], ACT.Sqrt).then_inc(d["root"], 1)
                        act.wait_ge(d["for_root"], i * 2 + 2)
                        nc.scalar.activation(small[:, 5, :], small[:, 4, :], ACT.Sqrt).then_inc(d["root"], 1)

                rounds(act, NSEPT, step)
            d = lay[2]
            act.wait_ge(srt[1]["loaded"], 16)
            for q in range(4):
                act.wait_ge(lay[1]["gath"][q], SORTS[0].tiles // 4 * 16)
                act.wait_ge(lay[1]["sel"][q], T0[2])
                act.wait_ge(lay[1]["mm"][q], T0[2])
            def records(i):
                nc.scalar.activation(rringf[:, :, 1:4], Sf[1][:, bass.ds(i * RING, RING), 1:4], ACT.Copy).then_inc(d["rec"][0], 1)

            def indices(i, q):
                nc.scalar.activation(idx[:, q * QUART:(q + 1) * QUART], S[1][:, bass.ds(i * RING + q * QUART, QUART), 0], ACT.Copy).then_inc(d["idx"][q], 1)

            def relations(i):
                act.wait_ge(d["relT"], i + 1)
                nc.scalar.activation(relT.rearrange("p a b -> p (a b)"), bank(0), ACT.Copy).then_inc(d["relTc"], 1)

            def step(i, ahead):
                if ahead:
                    act.wait_ge(d["coefn"], i + 1)
                    records(i + 1)
                for q in range(4):
                    if ahead:
                        act.wait_ge(d["gath"][q], i * (QUART * 16) + QUART * 16)
                        indices(i + 1, q)
                    if q == 1 and ahead:
                        relations(i + 1)
                    if q == 0:
                        if due(i):
                            act.wait_ge(d["w"], i)
                    for k in range(2):
                        act.wait_ge(d["mm"][q], i * QUART + (T0[2] + 2 * k + 2))
                        t = q * QUART + 2 * k
                        nc.scalar.activation(Ub[:, :, t:t + 2, :].rearrange("p b t j -> p t b j"),
                                             bank(2 + 2 * (q % 2) + k).rearrange("p (t b j) -> p t b j", t=2, j=W1), ACT.Copy).then_inc(d["uc"], 1)

            records(0)
            for q in range(4):
                indices(0, q)
            relations(0)
            rounds_ahead(act, ROUNDS[2], step)
            for q in range(4):
                act.wait_ge(d["add"][q], T0[3])
            def step(i):
                if due(i):
                    act.wait_ge(d["tr"], i)
                nc.scalar.activation(nst, reprT[:, bass.ds(i * (SEPT * P), SEPT * P)], ACT.Relu, bias=brel_c[:, 0:1]).then_inc(d["nst"], 1)
                act.wait_ge(d["for_root"], i + 1)
                nc.scalar.activation(small[:, 5, :], small[:, 4, :], ACT.Sqrt).then_inc(d["root"], 1)

            rounds(act, NSEPT, step)

        @block.tensor
        def _(pe):
            pe.wait_ge(s_const, 3)
            pe.wait_ge(s_ones, 2)
            for s, st in enumerate(SORTS):
                d = srt[s]
                acc = bank(s, st.cells)
                pe.wait_ge(d["blank"], 1)
                nc.tensor.matmul(acc, onesf[0:1, :], start[0:1, 0:st.cells], start=True, stop=True, skip_group_check=True).then_inc(d["opened"], 1)
                def step(i):
                    for k in range(2):
                        pe.wait_ge(d["count_oh"], i * 2 + k + 1)
                        nc.tensor.matmul(acc, ones[:], oh[:, k, 0:st.cells], start=False, stop=True, skip_group_check=True).then_inc(d["counted"], 1)

                rounds(pe, st.groups // 2, step)
                pe.wait_ge(d["marks"], 1)
                for c in range(up(st.tiles, 512) // 512):
                    n = min(512, st.tiles - c * 512)
                    for j in range(st.chunks):
                        nc.tensor.matmul(bank(2 + c, n), ones[:], mark[j][:, c * 512:c * 512 + n], start=(j == 0), stop=(j == st.chunks - 1)).then_inc(d["marked"], 1)
                pe.wait_ge(d["start"], 1)
                nc.tensor.matmul(acc, onesf[0:1, :], start[0:1, 0:st.cells], start=True, stop=True, skip_group_check=True).then_inc(d["opened"], 1)
                def step(i):
                    for k in range(2):
                        pe.wait_ge(d["oh"], i * 2 + k + 1)
                        nc.tensor.matmul(acc, strict[:], oh[:, k, 0:st.cells], start=False, stop=True, skip_group_check=True).then_inc(d["ranked"], 1)
                        pe.wait_ge(d["prod"], i * 2 + k + 1)
                        nc.tensor.matmul(acc, comp[:], oh[:, k, 0:st.cells], start=False, stop=True, skip_group_check=True).then_inc(d["summed"], 1)

                rounds(pe, st.groups // 2, step)
            pe.wait_ge(s_small, N_SMALL)
            for j in range(4):
                last = nc.tensor.transpose(bank(7, P, j * P), wtmp[:, j, :], ident[:])
            last.then_inc(s_wt, 1)
            pe.wait_ge(s_wtc, 1)
            for l in range(2):
                d = lay[l]
                def step(i):
                    for q in range(4):
                        pe.wait_ge(d["sel"][q], i * QUART + (QUART + T0[l]))
                        if due(i * QUART + T0[l]):
                            pe.wait_ge(d["add"][q], i * QUART + T0[l])
                        pe.wait_ge(d["gath"][q], i * (QUART * 16) + QUART * 16)
                        for t in range(q * QUART, (q + 1) * QUART):
                            nc.tensor.matmul(sums(t), sel[:, t, :], G[:, t, :], start=True, stop=True).then_inc(d["mm"][q], 1)

                rounds(pe, SORTS[0].tiles // RING, step)
                for q in range(4):
                    pe.wait_ge(d["add"][q], T0[l + 1])
                def step(i):
                    pe.wait_ge(d["xst"], i + 1)
                    pe.wait_ge(d["nst"], i + 1)
                    for j in range(SEPT):
                        nc.tensor.transpose(PS[:, j * P:(j + 1) * P], xst[:, j * D:(j + 1) * D], ident[:])
                        last = nc.tensor.transpose(PS[:, 1024 + j * P:1024 + (j + 1) * P], nst[:, j * D:(j + 1) * D], ident[:])
                    last.then_inc(d["tr"], 1)
                    pe.wait_ge(d["trc"], i + 1)
                    if due(i):
                        pe.wait_ge(d["stored" if l == 0 else "relu"], i)
                    for j in range(SEPT):
                        o = PS[:, 2048 + j * D:2048 + (j + 1) * D]
                        nc.tensor.matmul(o, xnT[:, j * D:(j + 1) * D], WT_sb[:, 2 * l, :], start=True, stop=False)
                        nc.tensor.matmul(o, xnT[:, (SEPT + j) * D:(SEPT + j + 1) * D], WT_sb[:, 2 * l + 1, :], start=False, stop=False)
                        last = nc.tensor.matmul(o, onesf[:], bias[:, l, :], start=False, stop=True)
                    last.then_inc(d["lin"], 1)

                rounds(pe, NSEPT, step)
                pe.wait_ge(d["stored"], NSEPT)
            d = lay[2]
            def relations(i):
                pe.wait_ge(d["rel"], i + 1)
                for q in range(4):
                    last = nc.tensor.transpose(bank(0, P, q * P), rel[:, q * QUART:(q + 1) * QUART, :].rearrange("p a b -> p (a b)"), ident[:])
                last.then_inc(d["relT"], 1)

            def coefficients(i):
                pe.wait_ge(d["relTc"], i + 1)
                for q in range(4):
                    last = nc.tensor.matmul(bank(1, 32, q * 32), relT[:, q, :], wcd[:].rearrange("p a b -> p (a b)"), start=True, stop=True)
                last.then_inc(d["coef"], 1)

            def step(i, ahead):
                for q in range(4):
                    pe.wait_ge(d["cmat"], i * 4 + q + 1)
                    if due(i * 8 + max(0, (q - 1) * 2)):
                        pe.wait_ge(d["uc"], i * 8 + max(0, (q - 1) * 2))
                    pe.wait_ge(d["gath"][q], i * (QUART * 16) + QUART * 16)
                    for k in range(QUART):
                        t = q * QUART + k
                        nc.tensor.matmul(bank(2 + 2 * (q % 2) + k // 2, 256, (k % 2) * 256), G[:, t, 0:D],
                                         C[:, t, :, :].rearrange("p b j -> p (b j)"), start=True, stop=True).then_inc(d["mm"][q], 1)
                    if q == 0 and ahead:
                        relations(i + 1)
                    if q == 1 and ahead:
                        coefficients(i + 1)
                pe.wait_ge(d["uc"], i * 8 + 8)
                pe.wait_ge(d["add"][3], i * 4 + T0[2])
                for b in range(BASES):
                    last = nc.tensor.matmul(bank(6), Wr[:, b, :], Ub[:, b, :, :].rearrange("p t j -> p (t j)"), start=(b == 0), stop=(b == BASES - 1))
                last.then_inc(d["w"], 1)

            relations(0)
            coefficients(0)
            rounds_ahead(pe, ROUNDS[2], step)

            def step(i):
                pe.wait_ge(d["nst"], i + 1)
                if due(i):
                    pe.wait_ge(d["relu"], i)
                for j in range(SEPT):
                    last = nc.tensor.transpose(PS[:, j * P:(j + 1) * P], nst[:, j * P:(j + 1) * P], ident[:])
                last.then_inc(d["tr"], 1)

            rounds(pe, NSEPT, step)

        @block.vector
        def _(dve):
            n_chain = [0]

            def link(ins):
                n_chain[0] += 1
                ins.then_inc(s_dve, 1)
                dve.wait_ge(s_dve, n_chain[0])

            def layernorm(link, bc, d, root, Xi):
                link(nc.vector.tensor_reduce(small[:, 3, :], y, AX, ALU.add))
                link(nc.vector.tensor_scalar(small[:, 3, :], small[:, 3, :], 1.0 / D, None, ALU.mult))
                link(nc.vector.tensor_tensor(y, y, bc(small[:, 3, :]), ALU.subtract))
                link(nc.vector.tensor_tensor(sq, y, y, ALU.mult))
                link(nc.vector.tensor_reduce(small[:, 4, :], sq, AX, ALU.add))
                nc.vector.tensor_scalar(small[:, 4, :], small[:, 4, :], 1.0 / D, EPS_LN, ALU.mult, ALU.add).then_inc(d["for_root"], 1)
                dve.wait_ge(d["root"], root)
                link(nc.vector.reciprocal(small[:, 5, :], small[:, 5, :]))
                nc.vector.tensor_tensor(Xi, y, bc(small[:, 5, :]), ALU.mult).then_inc(d["stored"], 1)

            nc.vector.memset(ones[:], 1.0).then_inc(s_ones, 1)
            nc.vector.memset(onesf[:], 1.0).then_inc(s_ones, 1)
            link(nc.vector.memset(keys[:, :, COLS:], 0.0))
            dve.wait_ge(s_iota, 2)
            link(nc.vector.tensor_copy(iota_b[:], iota_i[:]))
            link(nc.vector.tensor_copy(iota_f[:], iota_i[:, 0:P]))
            dve.wait_ge(s_const, 3)
            dve.wait_ge(s_edges, N_EDGES)

            for s, st in enumerate(SORTS):
                d = srt[s]
                B, L = st.wide, st.lanes
                acc = bank(s, st.cells)

                def cells(t):
                    return t[:, 0:st.cells].rearrange("p (l b) -> p l b", b=B)

                def onehot(k, g):
                    return nc.vector.tensor_tensor(
                        cells(oh[:, k, :]), iota_b[:, 0:B].unsqueeze(1).to_broadcast([P, L, B]),
                        keys[:, s, bass.ds(g * L, L)].unsqueeze(2).to_broadcast([P, L, B]), ALU.is_equal)

                node = raw[:, (SRC, DST)[s], :]
                link(nc.vector.tensor_scalar(kt, node, st.shift, None, ALU.logical_shift_right))
                link(nc.vector.tensor_scalar(kl, node, st.window - 1, None, ALU.bitwise_and))
                link(nc.vector.tensor_copy(keys[:, s, 0:COLS], kt))
                nc.vector.tensor_copy(locs[:, s, :], kl).then_inc(d["keys"], 1)
                dve.wait_ge(d["keys"], 1)
                nc.vector.memset(start[:], 0.0).then_inc(d["blank"], 1)
                dve.wait_ge(d["opened"], 1)
                def step(i):
                    for k in range(2):
                        if due(i * 2):
                            dve.wait_ge(d["counted"], i * 2)
                        onehot(k, i * 2 + k).then_inc(d["count_oh"], 1)

                rounds(dve, st.groups // 2, step)
                dve.wait_ge(d["counted"], st.groups)
                tiles, incl, ones_r, first = (tot[:, j, 0:st.bins] for j in range(4))
                link(nc.vector.tensor_copy(prod[:, 0:st.cells], acc))
                link(nc.vector.tensor_reduce(tiles, cells(prod).rearrange("p l b -> p b l")[:, 0:st.bins, :], AX, ALU.add))
                link(nc.vector.tensor_scalar(toti[:, 0:st.bins], tiles, float(P - 1), None, ALU.add))
                link(nc.vector.tensor_scalar(toti[:, 0:st.bins], toti[:, 0:st.bins], 7, None, ALU.logical_shift_right))
                link(nc.vector.tensor_copy(tiles, toti[:, 0:st.bins]))
                link(nc.vector.memset(ones_r, 1.0))
                link(nc.vector.tensor_tensor_scan(incl, ones_r, tiles, 0.0, ALU.mult, ALU.add))
                link(nc.vector.tensor_tensor(first, incl, tiles, ALU.subtract))
                sl = cells(start)
                link(nc.vector.memset(sl[:, :, st.bins:B], TRASH))
                link(nc.vector.tensor_scalar(sl[:, 0, 0:st.bins], first, float(P), None, ALU.mult))
                for j in range(1, L):
                    link(nc.vector.tensor_tensor(sl[:, j, 0:st.bins], sl[:, j - 1, 0:st.bins], cells(prod)[:, j - 1, 0:st.bins], ALU.add))
                for j in range(st.chunks):
                    nb = min(P, st.bins - 1 - j * P)
                    link(nc.vector.memset(prod[:, 0:P], 1e9))
                    link(nc.vector.tensor_copy(prod[:, 0:nb], incl[:, j * P:j * P + nb]))
                    link(nc.vector.tensor_tensor(prod[:, P:2 * P], prod[:, 0:P], ident[:], ALU.mult))
                    link(nc.vector.tensor_reduce(col[:, j:j + 1], prod[:, P:2 * P], AX, ALU.add))
                    link(nc.vector.tensor_scalar(mark[j][:, 0:st.tiles], tiota[:, 0:st.tiles], col[:, j:j + 1], None, ALU.is_ge))
                nc.vector.memset(posi[:, 0, 0:1], 0).then_inc(d["marks"], 1)
                nc.vector.memset(posi[:, 1, 0:1], 0).then_inc(d["start"], 1)
                for c in range(up(st.tiles, 512) // 512):
                    n = min(512, st.tiles - c * 512)
                    dve.wait_ge(d["marked"], st.chunks * (c + 1))
                    link(nc.vector.tensor_copy(table[32 * s:32 * s + 1, c * 512:c * 512 + n], PS[0:1, (2 + c) * 512:(2 + c) * 512 + n]))
                dve.wait_ge(d["opened"], 2)
                onehot(0, 0).then_inc(d["oh"], 1)
                if s:
                    scattered(dve, 0)
                per = st.per_half
                def step(i):
                    for h in range(2):
                        for j in range(per):
                            g = h * per + j
                            if due(i * (2 * per) + g):
                                dve.wait_ge(d["summed"], i * (2 * per) + g)
                            onehot((g + 1) % 2, i * (2 * per) + g + 1).then_inc(d["oh"], 1)
                            if due(i * (2 * per) + g):
                                dve.wait_ge(d["pos"], i * (2 * per) + g)
                            dve.wait_ge(d["ranked"], i * (2 * per) + g + 1)
                            nc.vector.tensor_tensor(prod[:, 0:st.cells], acc, oh[:, g % 2, 0:st.cells], ALU.mult).then_inc(d["prod"], 1)
                            dve.wait_ge(d["prod"], i * (2 * per) + g + 1)
                            with nc.allow_low_precision(reason="whole numbers, exact in float32"):
                                nc.vector.tensor_reduce(posi[:, 0, j * L:(j + 1) * L], cells(prod), AX, ALU.add).then_inc(d["pos"], 1)
                        dve.wait_ge(d["pos"], i * (2 * per) + (h + 1) * per)
                        nc.vector.tensor_scalar(posi[:, 1, :], posi[:, 0, :], P - 1, None, ALU.bitwise_and).then_inc(d["split"], 1)
                        nc.vector.tensor_scalar(posi[:, 2, :], posi[:, 0, :], 7, None, ALU.logical_shift_right).then_inc(d["split"], 1)
                        dve.wait_ge(d["split"], i * 4 + h * 2 + 2)
                        if due(i * (HALF * 16)):
                            dve.wait_ge(d["scat"][h], i * (HALF * 16))
                        nc.vector.scalar_tensor_tensor(idx[:, h * HALF:(h + 1) * HALF], posi[:, 1, :], float(st.tiles), posi[:, 2, :], ALU.mult, ALU.add).then_inc(d["idx"], 1)

                rounds(dve, COLS // RING, step)
                dve.wait_ge(d["summed"], st.groups)
                dve.wait_ge(d["oh"], st.groups + 1)

            def bc(t):
                return t.unsqueeze(2).to_broadcast([P, SEPT, D])

            dve.wait_ge(s_preset, 6)
            scattered(dve, 1)
            for l in range(2):
                d = lay[l]
                if l:
                    dve.wait_ge(lay[0]["nst"], NSEPT)
                link(nc.vector.memset(agg, 0.0))
                def step(i):
                    for q in range(4):
                        dve.wait_ge(d["rec"][q], i + (1 + R0[l]))
                        if due(i * QUART + T0[l]):
                            dve.wait_ge(d["mm"][q], i * QUART + T0[l])
                        for t in range(q * QUART, (q + 1) * QUART):
                            nc.vector.tensor_scalar(sel[:, t, :], iota_f[:], rringf[:, t, 1:2], rringf[:, t, 2:3], ALU.is_equal, ALU.mult).then_inc(d["sel"][q], 1)
                        for k in range(QUART):
                            t = q * QUART + k
                            blk = dve.value_load(table[0:1, bass.ds(i * RING + t, 1)], min_val=0, max_val=NBLK - 1)
                            a = agg[:, bass.ds(blk, 1), :].rearrange("p a c -> p (a c)")
                            dve.wait_ge(d["mm"][q], i * QUART + (T0[l] + k // 2 * 2 + 2))
                            if k:
                                if due(i * QUART + (T0[l] + k)):
                                    dve.wait_ge(d["add"][q], i * QUART + (T0[l] + k))
                            elif q:
                                dve.wait_ge(d["add"][q - 1], i * QUART + (T0[l] + QUART))
                            else:
                                if due(i * QUART + T0[l]):
                                    dve.wait_ge(d["add"][3], i * QUART + T0[l])
                            nc.vector.tensor_tensor(a, a, sums(t), ALU.add).then_inc(d["add"][q], 1)

                rounds(dve, SORTS[0].tiles // RING, step)
                dve.wait_ge(d["add"][3], T0[l + 1])
                def step(i):
                    per = (2, 13)[l]
                    n = [0]

                    def nlink(ins):
                        n[0] += 1
                        ins.then_inc(d["nchain"], 1)
                        dve.wait_ge(d["nchain"], i * per + n[0])

                    a = agg[:, bass.ds(i * SEPT, SEPT), :]
                    if due(i):
                        dve.wait_ge(d["nst"], i)
                    nlink(nc.vector.tensor_scalar(small[:, 6, :], a[:, :, D], EPS_WSUM, None, ALU.max))
                    nlink(nc.vector.reciprocal(small[:, 6, :], small[:, 6, :]))
                    if due(i):
                        dve.wait_ge(d["tr"], i)
                    nc.vector.tensor_tensor(nst.rearrange("p (b c) -> p b c", c=D), a[:, :, 0:D], bc(small[:, 6, :]), ALU.mult).then_inc(d["nst"], 1)
                    if l:
                        Xi = X[:, bass.ds(i * SEPT, SEPT), :]
                        dve.wait_ge(d["relu"], i + 1)
                        nlink(nc.vector.tensor_tensor(sq, y, y, ALU.mult))
                        nc.vector.tensor_reduce(small[:, 0, :], sq, AX, ALU.add).then_inc(d["for_root"], 1)
                        dve.wait_ge(d["root"], i * 2 + 1)
                        nlink(nc.vector.tensor_scalar(small[:, 2, :], small[:, 1, :], EPS_NORM, None, ALU.max))
                        nlink(nc.vector.reciprocal(small[:, 2, :], small[:, 2, :]))
                        nlink(nc.vector.tensor_tensor(y, y, bc(small[:, 2, :]), ALU.mult))
                        nlink(nc.vector.tensor_tensor(y, y, Xi, ALU.add))
                        layernorm(nlink, bc, d, i * 2 + 2, Xi)
                        dve.wait_ge(d["stored"], i + 1)
                    assert per - n[0] == 0, n

                rounds(dve, NSEPT, step)
            d = lay[2]
            dve.wait_ge(lay[1]["nst"], NSEPT)
            link(nc.vector.memset(reprT, 0.0))
            def spread(t, n):
                return t.unsqueeze(2).to_broadcast([P, RING, n])

            numbers = iota_f[:, 0:32].unsqueeze(1).to_broadcast([P, RING, 32])

            def relations(i):
                dve.wait_ge(d["rec"][0], i + (1 + R0[2]))
                nc.vector.tensor_tensor(rel, numbers, spread(rringf[:, :, 3], 32), ALU.is_equal).then_inc(d["rel"], 1)

            def coefficients(i):
                if due(i * 4):
                    dve.wait_ge(d["cmat"], i * 4)
                nc.vector.tensor_tensor(place, numbers, spread(rringf[:, :, 1], 32), ALU.is_equal).then_inc(d["node"], 1)
                dve.wait_ge(d["coef"], i + 1)
                nc.vector.tensor_tensor(cn, bank(1, P).rearrange("p (t b) -> p t b", b=BASES),
                                        spread(rringf[:, :, 2], BASES), ALU.mult).then_inc(d["coefn"], 1)

            def matrix(i, q):
                ks = slice(q * QUART, (q + 1) * QUART)
                dve.wait_ge(d["node"], i + 1)
                dve.wait_ge(d["coefn"], i + 1)
                dve.wait_ge(d["mm"][q], i * QUART + T0[2])
                nc.vector.tensor_tensor(C[:, ks, :, :], cn[:, ks, :].unsqueeze(3).to_broadcast([P, QUART, BASES, W1]),
                                        place[:, ks, :].unsqueeze(2).to_broadcast([P, QUART, BASES, W1]), ALU.mult).then_inc(d["cmat"], 1)

            def step(i, ahead):
                if ahead:
                    relations(i + 1)
                matrix(i, 2)
                matrix(i, 3)
                if ahead:
                    coefficients(i + 1)
                    matrix(i + 1, 0)
                    matrix(i + 1, 1)
                dve.wait_ge(d["w"], i + 1)
                for t in range(RING):
                    q, k = divmod(t, QUART)
                    win = dve.value_load(table[32:33, bass.ds(i * RING + t, 1)], min_val=0, max_val=SORTS[1].bins - 1)
                    a = reprT[:, bass.ds(win * W1, W1)]
                    if t == 0:
                        dve.wait_ge(d["add"][3], i * QUART + T0[2])
                    elif k:
                        dve.wait_ge(d["add"][q], i * QUART + (T0[2] + k))
                    else:
                        dve.wait_ge(d["add"][q - 1], i * QUART + (T0[2] + QUART))
                    nc.vector.tensor_tensor(a, a, bank(6, W1, t * W1), ALU.add).then_inc(d["add"][q], 1)

            relations(0)
            coefficients(0)
            matrix(0, 0)
            matrix(0, 1)
            rounds_ahead(dve, ROUNDS[2], step)

            def step(i):
                per = 6
                n = [0]

                def nlink(ins):
                    n[0] += 1
                    ins.then_inc(d["nchain"], 1)
                    dve.wait_ge(d["nchain"], i * per + n[0])

                Xi = X[:, bass.ds(i * SEPT, SEPT), :]
                dve.wait_ge(d["tr"], i + 1)
                nc.vector.tensor_tensor(y, PS[:, 0:SEPT * P].rearrange("p (b c) -> p b c", c=D), Xi, ALU.add).then_inc(d["relu"], 1)
                dve.wait_ge(d["relu"], i + 1)
                layernorm(nlink, bc, d, i + 1, Xi)
                dve.wait_ge(d["stored"], i + 1)
                assert per - n[0] == 0, n

            rounds(dve, NSEPT, step)


_INS = ["x", "src", "dst", "edge_type_32", "edge_weight", "edge_weight1", "L0_gnn_W1", "L0_gnn_b1",
        "L0_gnn_W2", "L0_gnn_b2", "L1_gnn_weight", "L1_gnn_w_comp", "L1_gnn_bias_param"]


def kernel(**inputs):
    import concourse.bacc as bacc
    from concourse.bass_utils import run_bass_kernel_spmd

    nc = bacc.Bacc("TRN2", target_bir_lowering=False, num_devices=1)
    arrays, args = {}, []
    for name in _INS:
        a = np.ascontiguousarray(inputs[name])
        if name == "edge_weight1":
            a = a.reshape(-1)
        arrays[f"in_{name}"] = a
        args.append(nc.dram_tensor(f"in_{name}", a.shape, mybir.dt.from_np(a.dtype), kind="ExternalInput").ap())
    args.append(nc.dram_tensor("out_0", (N, D), F32, kind="ExternalOutput").ap())
    build(nc, *args)
    return run_bass_kernel_spmd(nc, [arrays], core_ids=[0]).results[0]["out_0"]
```

```python
import numpy as np
import concourse.bass as bass
from concourse import mybir
from contextlib import ExitStack

P = 128
N, E, D = 6250, 200000, 128
RELS, BASES = 32, 8
NBLK = -(-N // P)
NPAD = NBLK * P
NFULL = N // P
NREST = N - NFULL * P
SEPT = 7
NSEPT = NBLK // SEPT
COLS = 1568
LAST = E - (P - 1) * COLS
RING = 16
HALF, QUART = 8, 4
EPS_WSUM, EPS_NORM, EPS_LN = 1e-12, 1e-12, 1e-5
TRASH = float(1 << 25)

F32, I32, F16 = mybir.dt.float32, mybir.dt.int32, mybir.dt.float16
ALU = mybir.AluOpType
ACT = mybir.ActivationFunctionType
AX = mybir.AxisListType.X


def up(n, m):
    return -(-n // m) * m


def due(count):
    return not (isinstance(count, int) and count == 0)


def rounds(eng, n, step):
    step(0)
    with eng.Fori(1, n) as i:
        step(i)


def rounds_ahead(eng, n, step):
    step(0, True)
    with eng.Fori(1, n - 1) as i:
        step(i, True)
    step(n - 1, False)


class Sort:

    def __init__(self, shift, lanes):
        self.shift, self.window = shift, 1 << shift
        self.bins = NPAD >> shift
        self.wide = self.bins + 1
        self.lanes = lanes
        self.cells = lanes * self.wide
        self.groups = COLS // lanes
        self.per_half = HALF // lanes
        self.tiles = up((E + self.bins * (P - 1)) // P, RING)
        self.chunks = up(self.bins, P) // P


SORTS = [Sort(7, 8), Sort(4, 1)]
W1 = SORTS[1].window
SPARE = SORTS[1].tiles - E // P + 1
LSORT = [0, 0, 1]
ROUNDS = [SORTS[s].tiles // RING for s in LSORT]
R0 = [0, ROUNDS[0], ROUNDS[0] + ROUNDS[1], sum(ROUNDS)]
T0 = [QUART * r for r in R0]


def build(nc, x, src, dst, etype, w, w1, W1m, b1, W2m, b2, Wrel, wcomp, brel, out):
    with ExitStack() as ctx:
        def sb(name, shape, dt=F32):
            return ctx.enter_context(nc.sbuf_tensor(name, shape, dt))

        def sem(name):
            return ctx.enter_context(nc.semaphore(name))

        rec_d = [nc.dram_tensor("rec_by_source", [P * SORTS[0].tiles, 4], I32).ap(),
                 nc.dram_tensor("rec_by_destination", [E + P * SPARE, 4], I32).ap()]
        h1_d = nc.dram_tensor("h1_table", [NPAD, D], F32).ap()
        x1_d = nc.dram_tensor("x1_table", [NPAD, D], F32).ap()

        raw = sb("raw", [P, 5, COLS], I32)
        SRC, DST, ET, WT, WT1 = range(5)
        rawf = raw[:].bitcast(F32)
        S = [sb(f"S{s}", [P, SORTS[s].tiles, 4], I32) for s in range(2)]
        Sf = [t[:].bitcast(F32) for t in S]
        natural = S[1][:, 0:COLS, :]
        X = sb("X", [P, NBLK, D])
        H1 = sb("H1", [P, NBLK, D])
        big = sb("big", [P, NBLK * (D + 1)])
        agg = big[:].rearrange("p (b c) -> p b c", c=D + 1)
        reprT = big[:, 0:NPAD]
        G = sb("G", [P, RING, D + 1])
        sel = sb("sel", [P, RING, P])
        ident = sb("ident", [P, P])
        strict = sb("strict", [P, P], F16)
        comp = sb("comp", [P, P], F16)
        ones = sb("ones", [P, P], F16)
        onesP = sb("onesP", [P, P])
        onesf = onesP[0:1, :]
        iota_i = sb("iota_i", [P, 400], I32)
        iota_b = sb("iota_b", [P, 400], F16)
        iota_f = sb("iota_f", [P, P])
        gflat = G[:].rearrange("p t c -> p (t c)")
        oh = gflat[:, 0:400].bitcast(F16).rearrange("p (k c) -> p k c", k=2)
        oh1 = gflat[:, 400:1200].bitcast(F16).rearrange("p (k c) -> p k c", k=4)
        prod = gflat[:, 1200:1600]
        start = gflat[:, 1600:2000]
        sflat = sel[:].rearrange("p t c -> p (t c)")
        tot = sflat[:, 0:1600].rearrange("p (k c) -> p k c", k=4)
        toti = sflat[:, 1600:2000].bitcast(I32)
        wrow = sb("wrow", [P, SORTS[1].tiles], F16)
        after = sb("after", [P, 1], I32)
        drops = sb("drops", [P, 4])
        flag = sb("flag", [1, 1], I32)
        pad = sb("pad", [P, 4, P], F16)
        col = sb("col", [P, 4])
        scratch = sb("scratch", [P, 2 * P])
        table = sb("table", [65, SORTS[1].tiles], I32)
        posi = sb("posi", [P, 3, HALF], I32)
        idx = sb("idx", [P, RING], I32)
        rring = sb("rring", [P, RING, 4], I32)
        rringf = rring[:].bitcast(F32)
        small = sb("small", [P, 8, SEPT])
        WT_sb = sb("WT_sb", [P, 4, D])
        bias = sb("bias", [1, 2, D])
        Wr = sb("Wr", [P, BASES, D])
        wcd = sb("wcd", [P, QUART, BASES])
        brel_c = sb("brel_c", [P, 1])

        early = H1[:].rearrange("p a b -> p (a b)")
        wtmp = H1[:, 0:4, :]
        kt = early[:, 512:512 + COLS].bitcast(I32)
        kl = early[:, 2112:2112 + COLS].bitcast(I32)
        tiota = early[:, 3712:3712 + SORTS[1].tiles]
        mark = [big[:, 0:1000].bitcast(F16)] + [early[:, 512 + 1000 * j:1512 + 1000 * j].bitcast(F16) for j in range(3)]
        keys = big[:, 2048:2048 + COLS + HALF].bitcast(F16).rearrange("p (s c) -> p s c", s=2)
        locs = big[:, 3648:3648 + COLS].bitcast(F16).rearrange("p (s c) -> p s c", s=2)
        flat = rawf.rearrange("p a c -> p (a c)")

        def stage(a, n):
            return flat[:, a * SEPT * D:(a + n) * SEPT * D]

        xst = stage(0, 1)
        nst = stage(1, 1)
        xnT = stage(2, 2)
        y = stage(4, 1).rearrange("p (b c) -> p b c", c=D)
        sq = stage(5, 1).rearrange("p (b c) -> p b c", c=D)
        C = H1[:, 0:16, :].rearrange("p a b -> p (a b)").rearrange("p (t b j) -> p t b j", b=BASES, j=W1)
        Ub = Sf[0][:, 0:512, :].rearrange("p t w -> p (t w)").rearrange("p (b t j) -> p b t j", t=RING, j=W1)
        rel = sel[:, 0:4, :].rearrange("p a b -> p (a b)").rearrange("p (t j) -> p t j", j=RELS)
        place = sel[:, 4:6, :].rearrange("p a b -> p (a b)").rearrange("p (t j) -> p t j", j=W1)
        relT = sel[:, 8:12, :]
        cn = sel[:, 12, :].rearrange("p (t b) -> p t b", b=BASES)

        PS = ctx.enter_context(nc.psum_tensor("PS", [P, 8 * 512], F32))

        def bank(b, n=512, off=0):
            return PS[:, b * 512 + off:b * 512 + off + n]

        def sums(t):
            return bank(t // 2, D + 1, (t % 2) * 256)

        s_tail = sem("tail_preset")
        s_preset = sem("areas_preset")
        s_edges = sem("edges_loaded")
        s_nodes = sem("nodes_loaded")
        s_small = sem("weights_loaded")
        s_rows = sem("rows_area_free")
        s_go = sem("pool_go")
        s_iota = sem("iota_made")
        s_filled = sem("masks_filled")
        s_const = sem("masks_made")
        s_ones = sem("ones_made")
        s_zeroed = sem("records_zeroed")
        s_dve = sem("dve_chain")
        s_wt = sem("weights_transposed")
        s_wtc = sem("weights_copied")
        s_out = sem("out_stored")
        srt = []
        for s in range(2):
            names = ["keys", "blank", "opened", "count_oh", "counted", "start", "marks", "marked",
                     "oh", "ranked", "prod", "summed", "pos", "split", "idx", "rec", "loaded",
                     "shaped", "linear", "local", "flag", "dropped", "dropsum", "offsets"]
            d = {n: sem(f"sort{s}_{n}") for n in names}
            d["scat"] = [sem(f"sort{s}_scat{h}") for h in range(2)]
            srt.append(d)
        shared = {n: [sem(f"ring_{n}{q}") for q in range(4)] for n in ("idx", "rec", "sel", "mm", "add")}
        lay = []
        for l in range(3):
            names = ["xst", "nst", "tr", "trc", "lin", "relu", "nchain", "for_root", "root",
                     "stored", "stored_dma"]
            if l == 2:
                names += ["rel", "relT", "relTc", "coef", "node", "coefn", "cmat", "w", "uc"]
            d = {n: sem(f"layer{l}_{n}") for n in names}
            d["gath"] = [sem(f"layer{l}_gath{q}") for q in range(4)]
            for n in shared:
                d[n] = shared[n]
            lay.append(d)

        N_EDGES, N_NODES, N_SMALL = 16 * 17, 32, 16 * (5 + QUART + 1)
        block = ctx.enter_context(nc.Block())

        def rows(t, b0, nb):
            return t[b0 * P:(b0 + nb) * P, :].rearrange("(b p) c -> p b c", p=P)

        def scattered(eng, s):
            for h in range(2):
                eng.wait_ge(srt[s]["scat"][h], COLS // 2 * 16)

        def registers(engine, row, i, most):
            return nc.values_load_multi_w_load_instructions(
                table[row:row + 1, bass.ds(i * RING, RING)], engines=(engine,), min_val=0, max_val=most,
                skip_runtime_bounds_check_because="the chip works the tables out from counts, which bound them")[1]

        def unsorted(eng):
            eng.wait_ge(srt[1]["flag"], 1)
            return eng.If(eng.value_load(flag[0:1, 0:1], min_val=0, max_val=E) > 0)

        @block.sync
        def _(sp):
            sp.wait_ge(s_tail, 3)
            for a, t in ((SRC, src), (WT, w), (DST, dst), (ET, etype), (WT1, w1)):
                view = raw[:] if a <= ET else rawf
                for p0, p1 in ((0, 112), (112, 127)):
                    sp.dma_start(view[p0:p1, a, :], t[p0 * COLS:p1 * COLS].rearrange("(p c) -> p c", c=COLS)).then_inc(s_edges, 16)
                sp.dma_start(view[127:128, a, 0:LAST], t[127 * COLS:E].rearrange("(p c) -> p c", p=1)).then_inc(s_edges, 16)
            with nc.allow_non_contiguous_dma(reason="127 words, once"):
                sp.dma_start(after[0:P - 2, :], dst[COLS:(P - 1) * COLS].rearrange("(p c) -> p c", c=COLS)[:, 0:1]).then_inc(s_edges, 16)
                sp.dma_start(after[P - 2:P - 1, :], dst[(P - 1) * COLS:(P - 1) * COLS + 1].rearrange("(p c) -> p c", c=1)).then_inc(s_edges, 16)
            sp.wait_ge(s_preset, 4)
            sp.dma_start(rec_d[0].rearrange("(p t) c -> p (t c)", p=P), S[0][:].rearrange("p t c -> p (t c)")).then_inc(s_zeroed, 16)
            sp.dma_start(rec_d[1][E:, :].rearrange("(p t) c -> p (t c)", p=P), S[0][:, 0:SPARE, :].rearrange("p t c -> p (t c)")).then_inc(srt[1]["linear"], 16)
            sp.dma_start(X[:, 0:NFULL, :], rows(x, 0, NFULL)).then_inc(s_nodes, 16)
            sp.dma_start(X[0:NREST, NFULL, :], x[NFULL * P:N, :]).then_inc(s_nodes, 16)
            sp.dma_start(H1[:, 0:2, :], W1m.rearrange("o (h i) -> o h i", h=2)).then_inc(s_small, 16)
            sp.dma_start(H1[:, 2:4, :], W2m.rearrange("o (h i) -> o h i", h=2)).then_inc(s_small, 16)
            sp.dma_start(bias[:, 0, :], b1.rearrange("(a c) -> a c", a=1)).then_inc(s_small, 16)
            sp.dma_start(bias[:, 1, :], b2.rearrange("(a c) -> a c", a=1)).then_inc(s_small, 16)
            sp.dma_start(Wr[:], Wrel.rearrange("b i o -> i b o")).then_inc(s_small, 16)
            for k in range(QUART):
                sp.dma_start(wcd[k * RELS:(k + 1) * RELS, k, :], wcomp).then_inc(s_small, 16)
            with nc.allow_non_contiguous_dma(reason="128 words, once"):
                sp.dma_start(brel_c[:], brel.rearrange("(p a) -> p a", a=1)).then_inc(s_small, 16)
            sp.wait_ge(srt[1]["shaped"], 4)
            for p0, p1 in ((0, 112), (112, 127)):
                sp.dma_start(rec_d[1][p0 * COLS:p1 * COLS, :].rearrange("(p t) c -> p (t c)", t=COLS), natural[p0:p1].rearrange("p t c -> p (t c)")).then_inc(srt[1]["linear"], 16)
            sp.dma_start(rec_d[1][127 * COLS:E, :].rearrange("(p t) c -> p (t c)", p=1), natural[127:128, 0:LAST, :].rearrange("p t c -> p (t c)")).then_inc(srt[1]["linear"], 16)
            scattered(sp, 0)
            sp.dma_start(S[0][:].rearrange("p t c -> p (t c)"), rec_d[0].rearrange("(p t) c -> p (t c)", p=P)).then_inc(srt[0]["loaded"], 16)
            sp.wait_ge(srt[1]["linear"], 64)
            with unsorted(sp):
                scattered(sp, 1)
            sp.wait_ge(srt[1]["offsets"], 1)

            def step(i):
                firsts = registers(mybir.EngineType.SP, 64, i, E + P * (SPARE - 1))
                for k in range(RING):
                    sp.dma_start(S[1][:, bass.ds(i * RING + k, 1), :].rearrange("p a c -> p (a c)"),
                                 rec_d[1][bass.ds(firsts[k], P), :]).then_inc(srt[1]["loaded"], 16)

            rounds(sp, ROUNDS[2], step)
            for l, (t, table_d) in enumerate(((H1, h1_d), (X, x1_d))):
                for i in range(NSEPT):
                    sp.wait_ge(lay[l]["stored"], i + 1)
                    sp.dma_start(rows(table_d, i * SEPT, SEPT), t[:, i * SEPT:(i + 1) * SEPT, :]).then_inc(lay[l]["stored_dma"], 16)
            for i in range(NSEPT):
                sp.wait_ge(lay[2]["stored"], i + 1)
                n = min(SEPT, NFULL - i * SEPT)
                sp.dma_start(rows(out, i * SEPT, n), X[:, i * SEPT:i * SEPT + n, :]).then_inc(s_out, 16)
            sp.dma_start(out[NFULL * P:N, :], X[0:NREST, NFULL, :]).then_inc(s_out, 16)
            sp.wait_ge(s_out, 16 * (NSEPT + 1))

        @block.gpsimd
        def _(pool):
            nc.gpsimd.memset(raw[:, 0:2, LAST:], NPAD).then_inc(s_tail, 1)
            nc.gpsimd.memset(raw[:, 2:5, LAST:], 0).then_inc(s_tail, 1)
            nc.gpsimd.memset(after[:], NPAD).then_inc(s_tail, 1)
            nc.gpsimd.iota(iota_i[:], [[1, 400]], base=0, channel_multiplier=0).then_inc(s_iota, 1)
            for m in (strict, comp, ident):
                nc.gpsimd.memset(m[:], 1.0).then_inc(s_filled, 1)
            pool.wait_ge(s_filled, 3)
            for m, op, sign in ((strict, ALU.is_gt, 1), (comp, ALU.is_ge, -1), (ident, ALU.is_equal, 1)):
                nc.gpsimd.affine_select(out=m[:], in_=m[:], compare_op=op, fill=0.0, base=0,
                                        pattern=[[sign, P]], channel_multiplier=-sign).then_inc(s_const, 1)
            nc.gpsimd.iota(tiota, [[1, SORTS[1].tiles]], base=0, channel_multiplier=0,
                           allow_small_or_imprecise_dtypes=True).then_inc(s_iota, 1)
            nc.gpsimd.memset(S[0][:], 0).then_inc(s_preset, 1)
            nc.gpsimd.memset(X[:, NFULL, :], 0.0).then_inc(s_preset, 1)
            nc.gpsimd.memset(wcd[:], 0.0).then_inc(s_preset, 1)
            nc.gpsimd.memset(small[:], 0.0).then_inc(s_preset, 1)
            def scatter(s, last):
                d = srt[s]

                def step(i):
                    for h in range(2):
                        pool.wait_ge(d["rec"], i * 8 + h * 4 + 4)
                        pool.wait_ge(d["idx"], i * 2 + h + 1)
                        pool.sem_inc(s_go, 1)
                        for k in range(h * HALF, (h + 1) * HALF):
                            pool.indirect_dma_start(
                                rec_d[s], bass.IndirectOffsetOnAxis(ap=idx[:, k:k + 1], axis=0),
                                rring[:, k, :], None, bounds_check=last,
                                oob_is_err=False).then_inc(d["scat"][h], 16)

                rounds(pool, COLS // RING, step)

            pool.wait_ge(s_zeroed, 16)
            scatter(0, P * SORTS[0].tiles - 1)
            pool.wait_ge(srt[1]["linear"], 64)
            with unsorted(pool):
                scatter(1, E - 1)
            pool.wait_ge(s_rows, 1)
            for l, tab in enumerate((x, h1_d, x1_d)):
                d = lay[l]
                if l:
                    pool.wait_ge(lay[l - 1]["stored_dma"], 16 * NSEPT)
                def step(i):
                    for q in range(4):
                        if due(i * QUART + T0[l]):
                            pool.wait_ge(d["mm"][q], i * QUART + T0[l])
                        pool.wait_ge(d["idx"][q], i + (1 + R0[l]))
                        pool.sem_inc(s_go, 1)
                        for k in range(q * QUART, (q + 1) * QUART):
                            pool.indirect_dma_start(
                                G[:, k, 0:D], None, tab,
                                bass.IndirectOffsetOnAxis(ap=idx[:, k:k + 1], axis=0)).then_inc(d["gath"][q], 16)

                rounds(pool, SORTS[LSORT[l]].tiles // RING, step)

        @block.scalar
        def _(act):
            words = (((raw[:, DST, :], locs[:, 0, :], rawf[:, WT, :], locs[:, 0, :]),
                      (raw[:, SRC, :], raw[:, DST, :], rawf[:, WT1, :], raw[:, ET, :])))

            def fill(s):
                d = srt[s]

                def step(i):
                    for h in range(2):
                        if due(i * (HALF * 16)):
                            act.wait_ge(d["scat"][h], i * (HALF * 16))
                        for wd, a in enumerate(words[s]):
                            to = (rringf if wd else rring)[:, h * HALF:(h + 1) * HALF, wd]
                            nc.scalar.activation(to, a[:, bass.ds(i * RING + h * HALF, HALF)], ACT.Copy).then_inc(d["rec"], 1)

                rounds(act, COLS // RING, step)

            act.wait_ge(s_edges, N_EDGES)
            act.wait_ge(srt[0]["keys"], 1)
            for wd, a in enumerate(words[1]):
                nc.scalar.activation((natural.bitcast(F32) if wd else natural)[:, :, wd], a, ACT.Copy).then_inc(srt[1]["shaped"], 1)
            fill(0)
            scattered(act, 0)
            with unsorted(act):
                fill(1)
                scattered(act, 1)
            act.wait_ge(s_nodes, N_NODES)
            act.wait_ge(s_wt, 1)
            nc.scalar.activation(WT_sb[:].rearrange("p a b -> p (a b)"), bank(7), ACT.Copy).then_inc(s_wtc, 1)
            for l in range(2):
                d = lay[l]
                if l == 0:
                    act.wait_ge(srt[0]["loaded"], 16)
                else:
                    for q in range(4):
                        act.wait_ge(lay[0]["gath"][q], SORTS[0].tiles // 4 * 16)
                        act.wait_ge(lay[0]["sel"][q], T0[1])
                def step(i):
                    for q in range(4):
                        ks = slice(q * QUART, (q + 1) * QUART)
                        frm = bass.ds(i * RING + q * QUART, QUART)
                        if due(i * (QUART * 16)):
                            act.wait_ge(d["gath"][q], i * (QUART * 16))
                        nc.scalar.activation(idx[:, ks], S[0][:, frm, 0], ACT.Copy).then_inc(d["idx"][q], 1)
                        if due(i * QUART + T0[l]):
                            act.wait_ge(d["sel"][q], i * QUART + T0[l])
                        nc.scalar.activation(rringf[:, ks, 1:3], Sf[0][:, frm, 1:3], ACT.Copy).then_inc(d["rec"][q], 1)

                rounds(act, SORTS[0].tiles // RING, step)
                def step(i):
                    if due(i):
                        act.wait_ge(d["tr"], i)
                    nc.scalar.activation(xst.rearrange("p (b c) -> p b c", c=D), (X, H1)[l][:, bass.ds(i * SEPT, SEPT), :], ACT.Copy).then_inc(d["xst"], 1)
                    if due(i):
                        act.wait_ge(d["lin"], i)
                    act.wait_ge(d["tr"], i + 1)
                    nc.scalar.activation(xnT.rearrange("p (h c) -> p h c", h=2),
                                         PS[:, 0:2048].rearrange("p (h c) -> p h c", h=2)[:, :, 0:SEPT * D], ACT.Copy).then_inc(d["trc"], 1)
                    act.wait_ge(d["lin"], i + 1)
                    if l == 0:
                        nc.scalar.activation(H1[:, bass.ds(i * SEPT, SEPT), :], PS[:, 2048:2048 + SEPT * D].rearrange("p (b c) -> p b c", c=D), ACT.Relu).then_inc(d["stored"], 1)
                    else:
                        if due(i):
                            act.wait_ge(d["stored"], i)
                        nc.scalar.activation(y, PS[:, 2048:2048 + SEPT * D].rearrange("p (b c) -> p b c", c=D), ACT.Relu).then_inc(d["relu"], 1)
                        act.wait_ge(d["for_root"], i * 2 + 1)
                        nc.scalar.activation(small[:, 1, :], small[:, 0, :], ACT.Sqrt).then_inc(d["root"], 1)
                        act.wait_ge(d["for_root"], i * 2 + 2)
                        nc.scalar.activation(small[:, 5, :], small[:, 4, :], ACT.Sqrt).then_inc(d["root"], 1)

                rounds(act, NSEPT, step)
            d = lay[2]
            act.wait_ge(srt[1]["local"], 1)
            for q in range(4):
                act.wait_ge(lay[1]["gath"][q], SORTS[0].tiles // 4 * 16)
                act.wait_ge(lay[1]["sel"][q], T0[2])
                act.wait_ge(lay[1]["mm"][q], T0[2])
            def records(i):
                nc.scalar.activation(rringf[:, :, 1:4], Sf[1][:, bass.ds(i * RING, RING), 1:4], ACT.Copy).then_inc(d["rec"][0], 1)

            def indices(i, q):
                nc.scalar.activation(idx[:, q * QUART:(q + 1) * QUART], S[1][:, bass.ds(i * RING + q * QUART, QUART), 0], ACT.Copy).then_inc(d["idx"][q], 1)

            def relations(i):
                act.wait_ge(d["relT"], i + 1)
                nc.scalar.activation(relT.rearrange("p a b -> p (a b)"), bank(0), ACT.Copy).then_inc(d["relTc"], 1)

            def step(i, ahead):
                if ahead:
                    act.wait_ge(d["coefn"], i + 1)
                    records(i + 1)
                for q in range(4):
                    if ahead:
                        act.wait_ge(d["gath"][q], i * (QUART * 16) + QUART * 16)
                        indices(i + 1, q)
                    if q == 1 and ahead:
                        relations(i + 1)
                    if q == 0:
                        if due(i):
                            act.wait_ge(d["w"], i)
                    act.wait_ge(d["mm"][q], i * QUART + (T0[2] + QUART))
                    nc.scalar.activation(Ub[:, :, q * QUART:(q + 1) * QUART, :].rearrange("p b t j -> p t b j"),
                                         bank(2 + q).rearrange("p (t b j) -> p t b j", t=QUART, j=W1), ACT.Copy).then_inc(d["uc"], 1)

            records(0)
            for q in range(4):
                indices(0, q)
            relations(0)
            rounds_ahead(act, ROUNDS[2], step)
            for q in range(4):
                act.wait_ge(d["add"][q], T0[3])
            def step(i):
                if due(i):
                    act.wait_ge(d["tr"], i)
                nc.scalar.activation(nst, reprT[:, bass.ds(i * (SEPT * P), SEPT * P)], ACT.Relu, bias=brel_c[:, 0:1]).then_inc(d["nst"], 1)
                act.wait_ge(d["for_root"], i + 1)
                nc.scalar.activation(small[:, 5, :], small[:, 4, :], ACT.Sqrt).then_inc(d["root"], 1)

            rounds(act, NSEPT, step)

        @block.tensor
        def _(pe):
            pe.wait_ge(s_const, 3)
            pe.wait_ge(s_ones, 2)
            def opening(s):
                nc.tensor.matmul(bank(s, SORTS[s].cells), onesf[0:1, :], start[0:1, 0:SORTS[s].cells], start=True, stop=True, skip_group_check=True).then_inc(srt[s]["opened"], 1)

            def count(s, rhs, number):
                pe.wait_ge(srt[s]["count_oh"], number)
                nc.tensor.matmul(bank(s, SORTS[s].cells), ones[:], rhs[:, 0:SORTS[s].cells], start=False, stop=True, skip_group_check=True).then_inc(srt[s]["counted"], 1)

            def windows(s):
                st = SORTS[s]
                pe.wait_ge(srt[s]["marks"], 1)
                for c in range(up(st.tiles, 512) // 512):
                    n = min(512, st.tiles - c * 512)
                    for j in range(st.chunks):
                        nc.tensor.matmul(bank(2 + c, n), ones[:], mark[j][:, c * 512:c * 512 + n], start=(j == 0), stop=(j == st.chunks - 1)).then_inc(srt[s]["marked"], 1)

            def rank(s, k, number):
                d, cells = srt[s], SORTS[s].cells
                pe.wait_ge(d["oh"], number)
                nc.tensor.matmul(bank(s, cells), strict[:], oh[:, k, 0:cells], start=False, stop=True, skip_group_check=True).then_inc(d["ranked"], 1)
                pe.wait_ge(d["prod"], number)
                nc.tensor.matmul(bank(s, cells), comp[:], oh[:, k, 0:cells], start=False, stop=True, skip_group_check=True).then_inc(d["summed"], 1)

            pe.wait_ge(srt[0]["blank"], 1)
            opening(0)
            opening(1)

            def step(i):
                for k in range(2):
                    count(0, oh[:, k, :], i * 2 + k + 1)

            rounds(pe, SORTS[0].groups // 2, step)
            windows(0)
            pe.wait_ge(srt[1]["dropped"], 1)
            nc.tensor.matmul(bank(7, 2), onesP[:], drops[:, 0:2], start=True, stop=True).then_inc(srt[1]["dropsum"], 1)
            pe.wait_ge(srt[0]["start"], 1)
            opening(0)

            def step(i):
                for h in range(2):
                    rank(0, h, i * 2 + h + 1)
                    for j in range(HALF):
                        count(1, oh1[:, j % 4, :], i * RING + h * HALF + j + 1)

            rounds(pe, SORTS[0].groups // 2, step)
            windows(1)
            for c in range(up(SORTS[1].tiles, 512) // 512):
                n = min(512, SORTS[1].tiles - c * 512)
                pe.wait_ge(srt[1]["split"], c + 1)
                for j in range(SORTS[1].chunks):
                    last = nc.tensor.matmul(bank(2 + c, n), pad[:, j, :], mark[j][:, c * 512:c * 512 + n], start=(j == 0), stop=(j == SORTS[1].chunks - 1))
                last.then_inc(srt[1]["marked"], 1)
            pe.wait_ge(srt[1]["start"], 1)
            with unsorted(pe):
                opening(1)

                def step(i):
                    for k in range(2):
                        rank(1, k, i * 2 + k + 1)

                rounds(pe, SORTS[1].groups // 2, step)
            pe.wait_ge(s_small, N_SMALL)
            for j in range(4):
                last = nc.tensor.transpose(bank(7, P, j * P), wtmp[:, j, :], ident[:])
            last.then_inc(s_wt, 1)
            pe.wait_ge(s_wtc, 1)
            for l in range(2):
                d = lay[l]
                def step(i):
                    for q in range(4):
                        pe.wait_ge(d["sel"][q], i * QUART + (QUART + T0[l]))
                        if due(i * QUART + T0[l]):
                            pe.wait_ge(d["add"][q], i * QUART + T0[l])
                        pe.wait_ge(d["gath"][q], i * (QUART * 16) + QUART * 16)
                        for t in range(q * QUART, (q + 1) * QUART):
                            nc.tensor.matmul(sums(t), sel[:, t, :], G[:, t, :], start=True, stop=True).then_inc(d["mm"][q], 1)

                rounds(pe, SORTS[0].tiles // RING, step)
                for q in range(4):
                    pe.wait_ge(d["add"][q], T0[l + 1])
                def step(i):
                    pe.wait_ge(d["xst"], i + 1)
                    pe.wait_ge(d["nst"], i + 1)
                    for j in range(SEPT):
                        nc.tensor.transpose(PS[:, j * P:(j + 1) * P], xst[:, j * D:(j + 1) * D], ident[:])
                        last = nc.tensor.transpose(PS[:, 1024 + j * P:1024 + (j + 1) * P], nst[:, j * D:(j + 1) * D], ident[:])
                    last.then_inc(d["tr"], 1)
                    pe.wait_ge(d["trc"], i + 1)
                    if due(i):
                        pe.wait_ge(d["stored" if l == 0 else "relu"], i)
                    for j in range(SEPT):
                        o = PS[:, 2048 + j * D:2048 + (j + 1) * D]
                        nc.tensor.matmul(o, xnT[:, j * D:(j + 1) * D], WT_sb[:, 2 * l, :], start=True, stop=False)
                        nc.tensor.matmul(o, xnT[:, (SEPT + j) * D:(SEPT + j + 1) * D], WT_sb[:, 2 * l + 1, :], start=False, stop=False)
                        last = nc.tensor.matmul(o, onesf[:], bias[:, l, :], start=False, stop=True)
                    last.then_inc(d["lin"], 1)

                rounds(pe, NSEPT, step)
                pe.wait_ge(d["stored"], NSEPT)
            d = lay[2]
            def relations(i):
                pe.wait_ge(d["rel"], i + 1)
                for q in range(4):
                    last = nc.tensor.transpose(bank(0, P, q * P), rel[:, q * QUART:(q + 1) * QUART, :].rearrange("p a b -> p (a b)"), ident[:])
                last.then_inc(d["relT"], 1)

            def coefficients(i):
                pe.wait_ge(d["relTc"], i + 1)
                for q in range(4):
                    last = nc.tensor.matmul(bank(1, 32, q * 32), relT[:, q, :], wcd[:].rearrange("p a b -> p (a b)"), start=True, stop=True)
                last.then_inc(d["coef"], 1)

            def step(i, ahead):
                for q in range(4):
                    pe.wait_ge(d["cmat"], i * 4 + q + 1)
                    if due(i * 4):
                        pe.wait_ge(d["uc"], i * 4)
                    pe.wait_ge(d["gath"][q], i * (QUART * 16) + QUART * 16)
                    for k in range(QUART):
                        t = q * QUART + k
                        nc.tensor.matmul(bank(2 + q, P, k * P), G[:, t, 0:D],
                                         C[:, t, :, :].rearrange("p b j -> p (b j)"), start=True, stop=True).then_inc(d["mm"][q], 1)
                    if q == 0 and ahead:
                        relations(i + 1)
                    if q == 1 and ahead:
                        coefficients(i + 1)
                pe.wait_ge(d["uc"], i * 4 + 4)
                pe.wait_ge(d["add"][3], i * 4 + T0[2])
                for b in range(BASES):
                    last = nc.tensor.matmul(bank(6, RING * W1), Wr[:, b, :], Ub[:, b, :, :].rearrange("p t j -> p (t j)"), start=(b == 0), stop=(b == BASES - 1))
                last.then_inc(d["w"], 1)

            relations(0)
            coefficients(0)
            rounds_ahead(pe, ROUNDS[2], step)

            def step(i):
                pe.wait_ge(d["nst"], i + 1)
                if due(i):
                    pe.wait_ge(d["relu"], i)
                for j in range(SEPT):
                    last = nc.tensor.transpose(PS[:, j * P:(j + 1) * P], nst[:, j * P:(j + 1) * P], ident[:])
                last.then_inc(d["tr"], 1)

            rounds(pe, NSEPT, step)

        @block.vector
        def _(dve):
            n_chain = [0]

            def link(ins):
                n_chain[0] += 1
                ins.then_inc(s_dve, 1)
                dve.wait_ge(s_dve, n_chain[0])

            def layernorm(link, bc, d, root, Xi):
                link(nc.vector.tensor_reduce(small[:, 3, :], y, AX, ALU.add))
                link(nc.vector.tensor_scalar(small[:, 3, :], small[:, 3, :], 1.0 / D, None, ALU.mult))
                link(nc.vector.tensor_tensor(y, y, bc(small[:, 3, :]), ALU.subtract))
                link(nc.vector.tensor_tensor(sq, y, y, ALU.mult))
                link(nc.vector.tensor_reduce(small[:, 4, :], sq, AX, ALU.add))
                nc.vector.tensor_scalar(small[:, 4, :], small[:, 4, :], 1.0 / D, EPS_LN, ALU.mult, ALU.add).then_inc(d["for_root"], 1)
                dve.wait_ge(d["root"], root)
                link(nc.vector.reciprocal(small[:, 5, :], small[:, 5, :]))
                nc.vector.tensor_tensor(Xi, y, bc(small[:, 5, :]), ALU.mult).then_inc(d["stored"], 1)

            nc.vector.memset(ones[:], 1.0).then_inc(s_ones, 1)
            nc.vector.memset(onesP[:], 1.0).then_inc(s_ones, 1)
            link(nc.vector.memset(keys[:, :, COLS:], 0.0))
            dve.wait_ge(s_iota, 2)
            link(nc.vector.tensor_copy(iota_b[:], iota_i[:]))
            link(nc.vector.tensor_copy(iota_f[:], iota_i[:, 0:P]))
            dve.wait_ge(s_const, 3)
            dve.wait_ge(s_edges, N_EDGES)

            def cells(s, t):
                return t[:, 0:SORTS[s].cells].rearrange("p (l b) -> p l b", b=SORTS[s].wide)

            def onehot(s, to, g):
                B, L = SORTS[s].wide, SORTS[s].lanes
                return nc.vector.tensor_tensor(
                    cells(s, to), iota_b[:, 0:B].unsqueeze(1).to_broadcast([P, L, B]),
                    keys[:, s, bass.ds(g * L, L)].unsqueeze(2).to_broadcast([P, L, B]), ALU.is_equal)

            def windows_of_edges(s):
                st, edge_node = SORTS[s], raw[:, (SRC, DST)[s], :]
                link(nc.vector.tensor_scalar(kt, edge_node, st.shift, None, ALU.logical_shift_right))
                link(nc.vector.tensor_copy(keys[:, s, 0:COLS], kt))
                if s == 0:
                    link(nc.vector.tensor_scalar(kl, edge_node, st.window - 1, None, ALU.bitwise_and))
                    nc.vector.tensor_copy(locs[:, s, :], kl).then_inc(srt[s]["keys"], 1)
                    dve.wait_ge(srt[s]["keys"], 1)

            def starts(s):
                st, d, L = SORTS[s], srt[s], SORTS[s].lanes
                tiles, incl, ones_r, first = (tot[:, j, 0:st.bins] for j in range(4))
                link(nc.vector.tensor_copy(prod[:, 0:st.cells], bank(s, st.cells)))
                counts = cells(s, prod)
                link(nc.vector.tensor_reduce(first, counts.rearrange("p l b -> p b l")[:, 0:st.bins, :], AX, ALU.add))
                link(nc.vector.tensor_scalar(toti[:, 0:st.bins], first, float(P - 1), None, ALU.add))
                link(nc.vector.tensor_scalar(toti[:, 0:st.bins], toti[:, 0:st.bins], 7, None, ALU.logical_shift_right))
                link(nc.vector.tensor_copy(tiles, toti[:, 0:st.bins]))
                link(nc.vector.memset(ones_r, 1.0))
                sl = cells(s, start)
                if s:
                    link(nc.vector.tensor_tensor_scan(incl, ones_r, first, 0.0, ALU.mult, ALU.add))
                    link(nc.vector.tensor_tensor(sl[:, 0, 0:st.bins], incl, first, ALU.subtract))
                    link(nc.vector.scalar_tensor_tensor(first, tiles, float(P), first, ALU.mult, ALU.subtract))
                    for j in range(st.chunks):
                        nb = min(P, st.bins - j * P)
                        link(nc.vector.memset(scratch[:, 0:P], 0.0))
                        link(nc.vector.tensor_copy(scratch[:, 0:nb], first[:, j * P:j * P + nb]))
                        link(nc.vector.tensor_tensor(scratch[:, P:2 * P], scratch[:, 0:P], ident[:], ALU.mult))
                        link(nc.vector.tensor_reduce(col[:, j:j + 1], scratch[:, P:2 * P], AX, ALU.add))
                        link(nc.vector.tensor_copy(pad[:, j, :], col[:, j:j + 1].to_broadcast([P, P])))
                link(nc.vector.tensor_tensor_scan(incl, ones_r, tiles, 0.0, ALU.mult, ALU.add))
                if s == 0:
                    link(nc.vector.tensor_tensor(first, incl, tiles, ALU.subtract))
                    link(nc.vector.tensor_scalar(sl[:, 0, 0:st.bins], first, float(P), None, ALU.mult))
                link(nc.vector.memset(sl[:, :, st.bins:], TRASH))
                for j in range(1, L):
                    link(nc.vector.tensor_tensor(sl[:, j, 0:st.bins], sl[:, j - 1, 0:st.bins], counts[:, j - 1, 0:st.bins], ALU.add))
                for j in range(st.chunks):
                    nb = min(P, st.bins - 1 - j * P)
                    link(nc.vector.memset(prod[:, 0:P], 1e9))
                    link(nc.vector.tensor_copy(prod[:, 0:nb], incl[:, j * P:j * P + nb]))
                    link(nc.vector.tensor_tensor(prod[:, P:2 * P], prod[:, 0:P], ident[:], ALU.mult))
                    link(nc.vector.tensor_reduce(col[:, j:j + 1], prod[:, P:2 * P], AX, ALU.add))
                    link(nc.vector.tensor_scalar(mark[j][:, 0:st.tiles], tiota[:, 0:st.tiles], col[:, j:j + 1], None, ALU.is_ge))
                nc.vector.memset(posi[:, 0, 0:1], 0).then_inc(d["marks"], 1)
                nc.vector.memset(posi[:, 1, 0:1], 0).then_inc(d["start"], 1)
                for c in range(up(st.tiles, 512) // 512):
                    n = min(512, st.tiles - c * 512)
                    dve.wait_ge(d["marked"], st.chunks * (c + 1))
                    link(nc.vector.tensor_copy(table[32 * s:32 * s + 1, c * 512:c * 512 + n], PS[0:1, (2 + c) * 512:(2 + c) * 512 + n]))
                    if s:
                        nc.vector.tensor_copy(wrow[:, c * 512:c * 512 + n], bank(2 + c, n)).then_inc(d["split"], 1)
                if s:
                    chunks = up(st.tiles, 512) // 512
                    for c in range(chunks):
                        n = min(512, st.tiles - c * 512)
                        dve.wait_ge(d["marked"], st.chunks * chunks + c + 1)
                        link(nc.vector.scalar_tensor_tensor(table[64:65, c * 512:c * 512 + n], tiota[64:65, c * 512:c * 512 + n], float(P),
                                                            PS[64:65, (2 + c) * 512:(2 + c) * 512 + n], ALU.mult, ALU.subtract))
                    nc.vector.memset(posi[:, 0, 0:1], 0).then_inc(d["offsets"], 1)

            def ranking(s, beside):
                st, d, L = SORTS[s], srt[s], SORTS[s].lanes
                acc, per = bank(s, st.cells), st.per_half
                dve.wait_ge(d["opened"], 2)
                onehot(s, oh[:, 0, :], 0).then_inc(d["oh"], 1)

                def step(i):
                    for h in range(2):
                        for j in range(per):
                            g = h * per + j
                            if due(i * (2 * per) + g):
                                dve.wait_ge(d["summed"], i * (2 * per) + g)
                            onehot(s, oh[:, (g + 1) % 2, :], i * (2 * per) + g + 1).then_inc(d["oh"], 1)
                            if due(i * (2 * per) + g):
                                dve.wait_ge(d["pos"], i * (2 * per) + g)
                            dve.wait_ge(d["ranked"], i * (2 * per) + g + 1)
                            nc.vector.tensor_tensor(prod[:, 0:st.cells], acc, oh[:, g % 2, 0:st.cells], ALU.mult).then_inc(d["prod"], 1)
                            beside(i, g)
                            dve.wait_ge(d["prod"], i * (2 * per) + g + 1)
                            with nc.allow_low_precision(reason="whole numbers, exact in float32"):
                                nc.vector.tensor_reduce(posi[:, 0, j * L:(j + 1) * L], cells(s, prod), AX, ALU.add).then_inc(d["pos"], 1)
                        dve.wait_ge(d["pos"], i * (2 * per) + (h + 1) * per)
                        here = idx[:, h * HALF:(h + 1) * HALF]
                        if s == 0:
                            nc.vector.tensor_scalar(posi[:, 1, :], posi[:, 0, :], P - 1, None, ALU.bitwise_and).then_inc(d["split"], 1)
                            nc.vector.tensor_scalar(posi[:, 2, :], posi[:, 0, :], 7, None, ALU.logical_shift_right).then_inc(d["split"], 1)
                            dve.wait_ge(d["split"], i * 4 + h * 2 + 2)
                        if due(i * (HALF * 16)):
                            dve.wait_ge(d["scat"][h], i * (HALF * 16))
                        if s == 0:
                            nc.vector.scalar_tensor_tensor(here, posi[:, 1, :], float(st.tiles), posi[:, 2, :], ALU.mult, ALU.add).then_inc(d["idx"], 1)
                        else:
                            nc.vector.tensor_copy(here, posi[:, 0, :]).then_inc(d["idx"], 1)
                            dve.wait_ge(d["idx"], i * 2 + h + 1)

                rounds(dve, COLS // RING, step)
                dve.wait_ge(d["summed"], st.groups)
                dve.wait_ge(d["oh"], st.groups + 1)

            windows_of_edges(0)
            nc.vector.memset(start[:], 0.0).then_inc(srt[0]["blank"], 1)
            dve.wait_ge(srt[0]["opened"], 1)

            def step(i):
                for k in range(2):
                    if due(i * 2):
                        dve.wait_ge(srt[0]["counted"], i * 2)
                    onehot(0, oh[:, k, :], i * 2 + k).then_inc(srt[0]["count_oh"], 1)

            rounds(dve, SORTS[0].groups // 2, step)
            dve.wait_ge(srt[0]["counted"], SORTS[0].groups)
            dve.wait_ge(srt[1]["opened"], 1)
            starts(0)
            windows_of_edges(1)
            link(nc.vector.tensor_tensor(locs[:, 1, 0:COLS - 1], keys[:, 1, 0:COLS - 1], keys[:, 1, 1:COLS], ALU.is_gt))
            link(nc.vector.tensor_reduce(drops[:, 0:1], locs[:, 1, 0:COLS - 1], AX, ALU.add))
            link(nc.vector.tensor_scalar(after[:], after[:], SORTS[1].shift, None, ALU.logical_shift_right))
            link(nc.vector.tensor_copy(drops[:, 2:3], after[:]))
            link(nc.vector.tensor_copy(drops[:, 3:4], keys[:, 1, COLS - 1:COLS]))
            link(nc.vector.tensor_tensor(drops[:, 1:2], drops[:, 3:4], drops[:, 2:3], ALU.is_gt))
            nc.vector.memset(posi[:, 0, 0:1], 0).then_inc(srt[1]["dropped"], 1)

            def counts_of_second(i, g):
                for j in range(HALF):
                    if j % 4 == 0 and due(i * RING + g * HALF + j):
                        dve.wait_ge(srt[1]["counted"], i * RING + g * HALF + j)
                    onehot(1, oh1[:, j % 4, :], i * RING + g * HALF + j).then_inc(srt[1]["count_oh"], 1)

            ranking(0, counts_of_second)
            dve.wait_ge(srt[1]["dropsum"], 1)
            link(nc.vector.tensor_reduce(drops[:, 2:3], bank(7, 2), AX, ALU.add))
            nc.vector.tensor_copy(flag[:], drops[0:1, 2:3]).then_inc(srt[1]["flag"], 1)
            dve.wait_ge(srt[1]["counted"], SORTS[1].groups)
            starts(1)
            with unsorted(dve):
                scattered(dve, 0)
                ranking(1, lambda i, g: None)
                scattered(dve, 1)

            def bc(t):
                return t.unsqueeze(2).to_broadcast([P, SEPT, D])

            dve.wait_ge(s_preset, 4)
            scattered(dve, 0)
            nc.vector.memset(G[:, :, D:D + 1], 1.0).then_inc(s_rows, 1)
            for l in range(2):
                d = lay[l]
                if l:
                    dve.wait_ge(lay[0]["nst"], NSEPT)
                link(nc.vector.memset(agg, 0.0))
                def selections(i, q):
                    dve.wait_ge(d["rec"][q], i + (1 + R0[l]))
                    if due(i * QUART + T0[l]):
                        dve.wait_ge(d["mm"][q], i * QUART + T0[l])
                    for t in range(q * QUART, (q + 1) * QUART):
                        nc.vector.tensor_scalar(sel[:, t, :], iota_f[:], rringf[:, t, 1:2], rringf[:, t, 2:3], ALU.is_equal, ALU.mult).then_inc(d["sel"][q], 1)

                def step(i, ahead):
                    blocks = registers(mybir.EngineType.DVE, 0, i, NBLK - 1)
                    for q in range(4):
                        if q < 3:
                            selections(i, q + 1)
                        elif ahead:
                            selections(i + 1, 0)
                        for k in range(QUART):
                            t = q * QUART + k
                            a = agg[:, bass.ds(blocks[t], 1), :].rearrange("p a c -> p (a c)")
                            dve.wait_ge(d["mm"][q], i * QUART + (T0[l] + k // 2 * 2 + 2))
                            if k:
                                if due(i * QUART + (T0[l] + k)):
                                    dve.wait_ge(d["add"][q], i * QUART + (T0[l] + k))
                            elif q:
                                dve.wait_ge(d["add"][q - 1], i * QUART + (T0[l] + QUART))
                            else:
                                if due(i * QUART + T0[l]):
                                    dve.wait_ge(d["add"][3], i * QUART + T0[l])
                            nc.vector.tensor_tensor(a, a, sums(t), ALU.add).then_inc(d["add"][q], 1)

                selections(0, 0)
                rounds_ahead(dve, SORTS[0].tiles // RING, step)
                dve.wait_ge(d["add"][3], T0[l + 1])
                def step(i):
                    per = (2, 13)[l]
                    n = [0]

                    def nlink(ins):
                        n[0] += 1
                        ins.then_inc(d["nchain"], 1)
                        dve.wait_ge(d["nchain"], i * per + n[0])

                    a = agg[:, bass.ds(i * SEPT, SEPT), :]
                    if due(i):
                        dve.wait_ge(d["nst"], i)
                    nlink(nc.vector.tensor_scalar(small[:, 6, :], a[:, :, D], EPS_WSUM, None, ALU.max))
                    nlink(nc.vector.reciprocal(small[:, 6, :], small[:, 6, :]))
                    if due(i):
                        dve.wait_ge(d["tr"], i)
                    nc.vector.tensor_tensor(nst.rearrange("p (b c) -> p b c", c=D), a[:, :, 0:D], bc(small[:, 6, :]), ALU.mult).then_inc(d["nst"], 1)
                    if l:
                        Xi = X[:, bass.ds(i * SEPT, SEPT), :]
                        dve.wait_ge(d["relu"], i + 1)
                        nlink(nc.vector.tensor_tensor(sq, y, y, ALU.mult))
                        nc.vector.tensor_reduce(small[:, 0, :], sq, AX, ALU.add).then_inc(d["for_root"], 1)
                        dve.wait_ge(d["root"], i * 2 + 1)
                        nlink(nc.vector.tensor_scalar(small[:, 2, :], small[:, 1, :], EPS_NORM, None, ALU.max))
                        nlink(nc.vector.reciprocal(small[:, 2, :], small[:, 2, :]))
                        nlink(nc.vector.tensor_tensor(y, y, bc(small[:, 2, :]), ALU.mult))
                        nlink(nc.vector.tensor_tensor(y, y, Xi, ALU.add))
                        layernorm(nlink, bc, d, i * 2 + 2, Xi)
                        dve.wait_ge(d["stored"], i + 1)
                    assert per - n[0] == 0, n

                rounds(dve, NSEPT, step)
            d = lay[2]
            dve.wait_ge(lay[1]["nst"], NSEPT)
            dve.wait_ge(srt[1]["loaded"], 16 * SORTS[1].tiles)
            nc.vector.scalar_tensor_tensor(Sf[1][:, :, 1], wrow[:], -float(W1), Sf[1][:, :, 1], ALU.mult, ALU.add).then_inc(srt[1]["local"], 1)
            link(nc.vector.memset(reprT, 0.0))
            def spread(t, n):
                return t.unsqueeze(2).to_broadcast([P, RING, n])

            def numbers(n):
                return iota_f[:, 0:n].unsqueeze(1).to_broadcast([P, RING, n])


            def relations(i):
                dve.wait_ge(d["rec"][0], i + (1 + R0[2]))
                nc.vector.tensor_tensor(rel, numbers(RELS), spread(rringf[:, :, 3], RELS), ALU.is_equal).then_inc(d["rel"], 1)

            def coefficients(i):
                if due(i * 4):
                    dve.wait_ge(d["cmat"], i * 4)
                nc.vector.tensor_tensor(place, numbers(W1), spread(rringf[:, :, 1], W1), ALU.is_equal).then_inc(d["node"], 1)
                dve.wait_ge(d["coef"], i + 1)
                nc.vector.tensor_tensor(cn, bank(1, P).rearrange("p (t b) -> p t b", b=BASES),
                                        spread(rringf[:, :, 2], BASES), ALU.mult).then_inc(d["coefn"], 1)

            def matrix(i, q):
                ks = slice(q * QUART, (q + 1) * QUART)
                dve.wait_ge(d["node"], i + 1)
                dve.wait_ge(d["coefn"], i + 1)
                dve.wait_ge(d["mm"][q], i * QUART + T0[2])
                nc.vector.tensor_tensor(C[:, ks, :, :], cn[:, ks, :].unsqueeze(3).to_broadcast([P, QUART, BASES, W1]),
                                        place[:, ks, :].unsqueeze(2).to_broadcast([P, QUART, BASES, W1]), ALU.mult).then_inc(d["cmat"], 1)

            def step(i, ahead):
                if ahead:
                    relations(i + 1)
                matrix(i, 2)
                matrix(i, 3)
                if ahead:
                    coefficients(i + 1)
                    matrix(i + 1, 0)
                    matrix(i + 1, 1)
                wins = registers(mybir.EngineType.DVE, 32, i, SORTS[1].bins - 1)
                dve.wait_ge(d["w"], i + 1)
                for t in range(RING):
                    q, k = divmod(t, QUART)
                    a = reprT[:, bass.ds(wins[t] * W1, W1)]
                    if t == 0:
                        dve.wait_ge(d["add"][3], i * QUART + T0[2])
                    elif k:
                        dve.wait_ge(d["add"][q], i * QUART + (T0[2] + k))
                    else:
                        dve.wait_ge(d["add"][q - 1], i * QUART + (T0[2] + QUART))
                    nc.vector.tensor_tensor(a, a, bank(6, W1, t * W1), ALU.add).then_inc(d["add"][q], 1)

            relations(0)
            coefficients(0)
            matrix(0, 0)
            matrix(0, 1)
            rounds_ahead(dve, ROUNDS[2], step)

            def step(i):
                per = 6
                n = [0]

                def nlink(ins):
                    n[0] += 1
                    ins.then_inc(d["nchain"], 1)
                    dve.wait_ge(d["nchain"], i * per + n[0])

                Xi = X[:, bass.ds(i * SEPT, SEPT), :]
                dve.wait_ge(d["tr"], i + 1)
                nc.vector.tensor_tensor(y, PS[:, 0:SEPT * P].rearrange("p (b c) -> p b c", c=D), Xi, ALU.add).then_inc(d["relu"], 1)
                dve.wait_ge(d["relu"], i + 1)
                layernorm(nlink, bc, d, i + 1, Xi)
                dve.wait_ge(d["stored"], i + 1)
                assert per - n[0] == 0, n

            rounds(dve, NSEPT, step)


_INS = ["x", "src", "dst", "edge_type_32", "edge_weight", "edge_weight1", "L0_gnn_W1", "L0_gnn_b1",
        "L0_gnn_W2", "L0_gnn_b2", "L1_gnn_weight", "L1_gnn_w_comp", "L1_gnn_bias_param"]


def kernel(**inputs):
    import concourse.bacc as bacc
    from concourse.bass_utils import run_bass_kernel_spmd

    nc = bacc.Bacc("TRN2", target_bir_lowering=False, num_devices=1)
    arrays, args = {}, []
    for name in _INS:
        a = np.ascontiguousarray(inputs[name])
        if name == "edge_weight1":
            a = a.reshape(-1)
        arrays[f"in_{name}"] = a
        args.append(nc.dram_tensor(f"in_{name}", a.shape, mybir.dt.from_np(a.dtype), kind="ExternalInput").ap())
    args.append(nc.dram_tensor("out_0", (N, D), F32, kind="ExternalOutput").ap())
    build(nc, *args)
    return run_bass_kernel_spmd(nc, [arrays], core_ids=[0]).results[0]["out_0"]
```

```python
import numpy as np
import concourse.bass as bass
from concourse import mybir
from contextlib import ExitStack

P = 128
N, E, D = 6250, 200000, 128
RELS, BASES = 32, 8
NBLK = -(-N // P)
NPAD = NBLK * P
NFULL = N // P
NREST = N - NFULL * P
SEPT = 7
NSEPT = NBLK // SEPT
COLS = 1568
LAST = E - (P - 1) * COLS
COUNT_COLS = 224
RING = 16
HALF, QUART = 8, 4
EPS_WSUM, EPS_NORM, EPS_LN = 1e-12, 1e-12, 1e-5
TRASH = float(1 << 25)

F32, I32, F16 = mybir.dt.float32, mybir.dt.int32, mybir.dt.float16
ALU = mybir.AluOpType
ACT = mybir.ActivationFunctionType
AX = mybir.AxisListType.X


def up(n, m):
    return -(-n // m) * m


def due(count):
    return not (isinstance(count, int) and count == 0)


def rounds(eng, n, step):
    step(0)
    with eng.Fori(1, n) as i:
        step(i)


def rounds_behind(eng, n, step):
    step(0, None, True)
    with eng.Fori(0, n - 2) as i:
        step(i + 1, i, True)
    step(n - 1, n - 2, False)


def rounds_ahead(eng, n, step):
    step(0, True)
    with eng.Fori(1, n - 1) as i:
        step(i, True)
    step(n - 1, False)


class Sort:

    def __init__(self, shift, lanes):
        self.shift, self.window = shift, 1 << shift
        self.bins = NPAD >> shift
        self.wide = self.bins + 1
        self.lanes = lanes
        self.cells = lanes * self.wide
        self.groups = COLS // lanes
        self.per_half = HALF // lanes
        self.tiles = up((E + self.bins * (P - 1)) // P, RING)
        self.chunks = up(self.bins, P) // P


SORTS = [Sort(7, 8), Sort(5, 2)]
DWIN = SORTS[1].window
SPARE = SORTS[1].tiles - E // P + 1
LSORT = [0, 0, 1]
ROUNDS = [SORTS[s].tiles // RING for s in LSORT]
R0 = [0, ROUNDS[0], ROUNDS[0] + ROUNDS[1], sum(ROUNDS)]
T0 = [QUART * r for r in R0]


def build(nc, x, src, dst, etype, w, w1, lin1, b1, lin2, b2, Wrel, wcomp, brel, out):
    with ExitStack() as ctx:
        def sb(name, shape, dt=F32):
            return ctx.enter_context(nc.sbuf_tensor(name, shape, dt))

        def sem(name):
            return ctx.enter_context(nc.semaphore(name))

        rec_d = [nc.dram_tensor("rec_by_source", [P * SORTS[0].tiles, 4], I32).ap(),
                 nc.dram_tensor("rec_by_destination", [E + P * SPARE, 4], I32).ap()]
        h1_d = nc.dram_tensor("h1_table", [NPAD, D], F32).ap()
        x1_d = nc.dram_tensor("x1_table", [NPAD, D], F32).ap()

        raw = sb("raw", [P, 5, COLS], I32)
        SRC, DST, ET, WT, WT1 = range(5)
        rawf = raw[:].bitcast(F32)
        S = [sb(f"S{s}", [P, SORTS[s].tiles, 4], I32) for s in range(2)]
        Sf = [t[:].bitcast(F32) for t in S]
        natural = S[1][:, 0:COLS, :]
        X = sb("X", [P, NBLK, D])
        H1 = sb("H1", [P, NBLK, D])
        big = sb("big", [P, NBLK * (D + 1)])
        agg = big[:].rearrange("p (b c) -> p b c", c=D + 1)
        reprT = big[:, 0:NPAD]
        G = sb("G", [P, RING, D + 1])
        sel = sb("sel", [P, RING, P])
        ident = sb("ident", [P, P])
        ident_h = sb("ident_h", [P, P], F16)
        strict = sb("strict", [P, P], F16)
        comp = sb("comp", [P, P], F16)
        ones = sb("ones", [P, P], F16)
        onesP = sb("onesP", [P, P])
        onesf = onesP[0:1, :]
        iota_i = sb("iota_i", [P, 400], I32)
        iota_b = sb("iota_b", [P, 400], F16)
        iota_f = sb("iota_f", [P, P])
        gflat = G[:].rearrange("p t c -> p (t c)")
        oh = gflat[:, 0:400].bitcast(F16).rearrange("p (k c) -> p k c", k=2)
        oh1 = gflat[:, 400:1200].bitcast(F16).rearrange("p (k c) -> p k c", k=4)
        prod = gflat[:, 1200:1600]
        start = gflat[:, 1600:2000]
        sflat = sel[:].rearrange("p t c -> p (t c)")
        tot = sflat[:, 0:1600].rearrange("p (k c) -> p k c", k=4)
        equal = sflat[:, 0:COLS].bitcast(F16).rearrange("p (k c) -> p k c", k=2)
        toti = sflat[:, 1600:2000].bitcast(I32)
        wrow = sb("wrow", [P, SORTS[1].tiles], F16)
        after = sb("after", [P, 1], I32)
        drops = sb("drops", [P, 4])
        flag = sb("flag", [1, 1], I32)
        pad = sb("pad", [P, 4, P], F16)
        col = sb("col", [P, 4])
        scratch = sb("scratch", [P, 2 * P])
        table = sb("table", [65, SORTS[1].tiles], I32)
        posi = sb("posi", [P, 3, HALF], I32)
        idx = sb("idx", [P, RING], I32)
        rring = sb("rring", [P, RING, 4], I32)
        rringf = rring[:].bitcast(F32)
        stats = sb("stats", [P, 7, SEPT])
        SQUARES, NORM, SUM, NEG_MEAN, DEVIATION, STD, INV_NORM = range(7)
        WT_sb = sb("WT_sb", [P, 4, D])
        bias = sb("bias", [1, 2, D])
        Wr = sb("Wr", [P, BASES, D])
        wcd = sb("wcd", [P, QUART, BASES])
        brel_c = sb("brel_c", [P, 1])
        rw = sb("rw", [P, NBLK])
        eps_ln = sb("eps_ln", [P, 1])

        early = H1[:].rearrange("p a b -> p (a b)")
        wtmp = H1[:, 0:4, :]
        kt = early[:, 512:512 + COLS].bitcast(I32)
        kl = early[:, 2112:2112 + COLS].bitcast(I32)
        tiota = early[:, 3712:3712 + SORTS[1].tiles]
        mark = [big[:, 0:1000].bitcast(F16)] + [early[:, 512 + 1000 * j:1512 + 1000 * j].bitcast(F16) for j in range(3)]
        keys = big[:, 2048:2048 + COLS + HALF].bitcast(F16).rearrange("p (s c) -> p s c", s=2)
        locs = big[:, 3648:3648 + COLS].bitcast(F16).rearrange("p (s c) -> p s c", s=2)
        flat = rawf.rearrange("p a c -> p (a c)")

        def stage(a, n):
            return flat[:, a * SEPT * D:(a + n) * SEPT * D]

        ownT = stage(0, 1)
        meanT = stage(1, 1)
        squares = stage(2, 1)
        relu2 = stage(3, 1)
        own_st = stage(4, 1)
        mean_st = stage(5, 1)
        C = H1[:, 0:BASES * DWIN // 8, :].rearrange("p a b -> p (a b)").rearrange("p (t b j) -> p t b j", b=BASES, j=DWIN)
        Ub = Sf[0][:, 0:RING * BASES * DWIN // 4, :].rearrange("p t w -> p (t w)").rearrange("p (b t j) -> p b t j", t=RING, j=DWIN)
        rel = sel[:, 0:2, :].rearrange("p a b -> p (a b)").bitcast(F16).rearrange("p (t j) -> p t j", j=RELS)
        place = sel[:, 4:4 + RING * DWIN // P, :].rearrange("p a b -> p (a b)").rearrange("p (t j) -> p t j", j=DWIN)
        relT = sel[:, 8:12, :]
        cn = sel[:, 12, :].rearrange("p (t b) -> p t b", b=BASES)

        PS = ctx.enter_context(nc.psum_tensor("PS", [P, 8 * 512], F32))

        def bank(b, n=512, off=0):
            return PS[:, b * 512 + off:b * 512 + off + n]

        def sums(t):
            return bank(t % HALF // 2, D + 1, (t % 2) * 256)

        def basis_sums(t, n=1):
            return bank(2 + t % HALF // 2, n * BASES * DWIN, t % 2 * BASES * DWIN)

        def lin(j=0, n=SEPT):
            return PS[:, 3072 + j * D:3072 + (j + n) * D]

        def trs(j=0, n=SEPT):
            return PS[:, 2048 + j * D:2048 + (j + n) * D]

        s_tail = sem("tail_preset")
        s_preset = sem("areas_preset")
        s_sources = sem("sources_loaded")
        s_edges = sem("edges_loaded")
        s_nodes = sem("nodes_loaded")
        s_small = sem("weights_loaded")
        s_rows = sem("rows_area_free")
        s_go = sem("pool_go")
        s_go_act = sem("scalar_go")
        s_go_dve = sem("vector_go")
        s_iota = sem("iota_made")
        s_filled = sem("masks_filled")
        s_const = sem("masks_made")
        s_ones = sem("ones_made")
        s_zeroed = sem("records_zeroed")
        s_dve = sem("dve_chain")
        s_wt = sem("weights_transposed")
        s_wtc = sem("weights_copied")
        s_out = sem("out_stored")
        srt = []
        for s in range(2):
            names = ["opened", "count_oh", "counted", "start", "marks", "marked", "oh", "ranked", "prod",
                     "summed", "pos", "split", "idx", "rec", "loaded"]
            names += [["keys", "blank", "reduced", "first"], ["shaped", "linear", "local", "flag", "dropped", "dropsum", "offsets"]][s]
            d = {n: sem(f"sort{s}_{n}") for n in names}
            d["scat"] = [sem(f"sort{s}_scat{h}") for h in range(2)]
            srt.append(d)
        shared = {n: [sem(f"ring_{n}{q}") for q in range(4)] for n in ("idx", "rec", "sel", "mm", "add")}
        lay = []
        for l in range(3):
            names = ["tr", "relu", "nchain", "for_root", "root", "squares", "stored", "stored_dma"]
            if l < 2:
                names += ["ownst", "meanst", "ownT", "ownTc", "ownlin", "own", "trc", "lin", "comb", "res"]
            else:
                names += ["nst","rel", "relT", "relTc", "coef", "node", "coefn", "cmat"]
            d = {n: sem(f"layer{l}_{n}") for n in names}
            if l == 2:
                d["w"] = [sem(f"bases_multiplied{h}") for h in range(2)]
                d["uc"] = [sem(f"basis_sums_copied{q}") for q in range(4)]
            d["gath"] = [sem(f"layer{l}_gath{q}") for q in range(4)]
            for n in shared:
                d[n] = shared[n]
            lay.append(d)

        N_EDGES, N_NODES, N_SMALL = 16 * 14, 32, 16 * (5 + QUART + 1)
        block = ctx.enter_context(nc.Block())

        def rows(t, b0, nb):
            return t[b0 * P:(b0 + nb) * P, :].rearrange("(b p) c -> p b c", p=P)

        def node(t, i, j):
            return t[:, bass.ds(i * SEPT + j, 1), :].rearrange("p a c -> p (a c)")

        def scattered(eng, s):
            for h in range(2):
                eng.wait_ge(srt[s]["scat"][h], COLS // 2 * 16)

        def registers(engine, row, i, most):
            return nc.values_load_multi_w_load_instructions(
                table[row:row + 1, bass.ds(i * RING, RING)], engines=(engine,), min_val=0, max_val=most,
                skip_runtime_bounds_check_because="the chip works the tables out from counts, which bound them")[1]

        def unsorted(eng):
            eng.wait_ge(srt[1]["flag"], 1)
            return eng.If(eng.value_load(flag[0:1, 0:1], min_val=0, max_val=E) > 0)

        @block.sync
        def _(sp):
            sp.wait_ge(s_tail, 3)
            for a, t in ((SRC, src), (WT, w), (DST, dst), (ET, etype), (WT1, w1)):
                view = raw[:] if a <= ET else rawf
                loaded = s_sources if a == SRC else s_edges
                for p0, p1 in ((0, 112), (112, 127)):
                    sp.dma_start(view[p0:p1, a, :], t[p0 * COLS:p1 * COLS].rearrange("(p c) -> p c", c=COLS)).then_inc(loaded, 16)
                sp.dma_start(view[127:128, a, 0:LAST], t[127 * COLS:E].rearrange("(p c) -> p c", p=1)).then_inc(loaded, 16)
            with nc.allow_non_contiguous_dma(reason="127 words, once"):
                sp.dma_start(after[0:P - 2, :], dst[COLS:(P - 1) * COLS].rearrange("(p c) -> p c", c=COLS)[:, 0:1]).then_inc(s_edges, 16)
                sp.dma_start(after[P - 2:P - 1, :], dst[(P - 1) * COLS:(P - 1) * COLS + 1].rearrange("(p c) -> p c", c=1)).then_inc(s_edges, 16)
            sp.wait_ge(s_preset, 4)
            sp.dma_start(rec_d[0].rearrange("(p t) c -> p (t c)", p=P), S[0][:].rearrange("p t c -> p (t c)")).then_inc(s_zeroed, 16)
            sp.dma_start(rec_d[1][E:, :].rearrange("(p t) c -> p (t c)", p=P), S[0][:, 0:SPARE, :].rearrange("p t c -> p (t c)")).then_inc(srt[1]["linear"], 16)
            sp.dma_start(X[:, 0:NFULL, :], rows(x, 0, NFULL)).then_inc(s_nodes, 16)
            sp.dma_start(X[0:NREST, NFULL, :], x[NFULL * P:N, :]).then_inc(s_nodes, 16)
            sp.dma_start(H1[:, 0:2, :], lin1.rearrange("o (h i) -> o h i", h=2)).then_inc(s_small, 16)
            sp.dma_start(H1[:, 2:4, :], lin2.rearrange("o (h i) -> o h i", h=2)).then_inc(s_small, 16)
            sp.dma_start(bias[:, 0, :], b1.rearrange("(a c) -> a c", a=1)).then_inc(s_small, 16)
            sp.dma_start(bias[:, 1, :], b2.rearrange("(a c) -> a c", a=1)).then_inc(s_small, 16)
            sp.dma_start(Wr[:], Wrel.rearrange("b i o -> i b o")).then_inc(s_small, 16)
            for k in range(QUART):
                sp.dma_start(wcd[k * RELS:(k + 1) * RELS, k, :], wcomp).then_inc(s_small, 16)
            with nc.allow_non_contiguous_dma(reason="128 words, once"):
                sp.dma_start(brel_c[:], brel.rearrange("(p a) -> p a", a=1)).then_inc(s_small, 16)
            sp.wait_ge(srt[1]["shaped"], 4)
            for p0, p1 in ((0, 112), (112, 127)):
                sp.dma_start(rec_d[1][p0 * COLS:p1 * COLS, :].rearrange("(p t) c -> p (t c)", t=COLS), natural[p0:p1].rearrange("p t c -> p (t c)")).then_inc(srt[1]["linear"], 16)
            sp.dma_start(rec_d[1][127 * COLS:E, :].rearrange("(p t) c -> p (t c)", p=1), natural[127:128, 0:LAST, :].rearrange("p t c -> p (t c)")).then_inc(srt[1]["linear"], 16)
            scattered(sp, 0)
            by_tile = rec_d[0].rearrange("(p t) c -> p t c", p=P)
            sp.dma_start(S[0][:, 0:RING, :], by_tile[:, 0:RING, :]).then_inc(srt[0]["first"], 16)
            sp.dma_start(S[0][:, RING:, :], by_tile[:, RING:, :]).then_inc(srt[0]["loaded"], 16)
            sp.wait_ge(srt[1]["linear"], 64)
            with unsorted(sp):
                scattered(sp, 1)
            sp.wait_ge(srt[1]["offsets"], 1)

            def step(i):
                firsts = registers(mybir.EngineType.SP, 64, i, E + P * (SPARE - 1))
                for k in range(RING):
                    sp.dma_start(S[1][:, bass.ds(i * RING + k, 1), :].rearrange("p a c -> p (a c)"),
                                 rec_d[1][bass.ds(firsts[k], P), :]).then_inc(srt[1]["loaded"], 16)

            rounds(sp, ROUNDS[2], step)
            for l, (t, table_d) in enumerate(((H1, h1_d), (X, x1_d))):
                for i in range(NSEPT):
                    sp.wait_ge(lay[l]["stored"], (i + 1) * (1, SEPT)[l])
                    sp.dma_start(rows(table_d, i * SEPT, SEPT), t[:, i * SEPT:(i + 1) * SEPT, :]).then_inc(lay[l]["stored_dma"], 16)
            for i in range(NSEPT):
                sp.wait_ge(lay[2]["stored"], (i + 1) * SEPT)
                n = min(SEPT, NFULL - i * SEPT)
                sp.dma_start(rows(out, i * SEPT, n), X[:, i * SEPT:i * SEPT + n, :]).then_inc(s_out, 16)
            sp.dma_start(out[NFULL * P:N, :], X[0:NREST, NFULL, :]).then_inc(s_out, 16)
            sp.wait_ge(s_out, 16 * (NSEPT + 1))

        @block.gpsimd
        def _(pool):
            nc.gpsimd.memset(raw[:, 0:2, LAST:], NPAD).then_inc(s_tail, 1)
            nc.gpsimd.memset(raw[:, 2:5, LAST:], 0).then_inc(s_tail, 1)
            nc.gpsimd.memset(after[:], NPAD).then_inc(s_tail, 1)
            nc.gpsimd.iota(iota_i[:], [[1, 400]], base=0, channel_multiplier=0).then_inc(s_iota, 1)
            for m in (strict, comp, ident):
                nc.gpsimd.memset(m[:], 1.0).then_inc(s_filled, 1)
            pool.wait_ge(s_filled, 3)
            for m, op, sign in ((strict, ALU.is_gt, 1), (comp, ALU.is_ge, -1), (ident, ALU.is_equal, 1)):
                nc.gpsimd.affine_select(out=m[:], in_=m[:], compare_op=op, fill=0.0, base=0,
                                        pattern=[[sign, P]], channel_multiplier=-sign).then_inc(s_const, 1)
            nc.gpsimd.iota(tiota, [[1, SORTS[1].tiles]], base=0, channel_multiplier=0,
                           allow_small_or_imprecise_dtypes=True).then_inc(s_iota, 1)
            nc.gpsimd.memset(S[0][:], 0).then_inc(s_preset, 1)
            nc.gpsimd.memset(X[:, NFULL, :], 0.0).then_inc(s_preset, 1)
            nc.gpsimd.memset(wcd[:], 0.0).then_inc(s_preset, 1)
            nc.gpsimd.memset(stats[:], 0.0).then_inc(s_preset, 1)
            def scatter(s, last):
                d = srt[s]

                def step(i):
                    for h in range(2):
                        pool.wait_ge(d["rec"], i * 8 + h * 4 + 4)
                        pool.wait_ge(d["idx"], i * 2 + h + 1)
                        pool.sem_inc(s_go, 1)
                        for k in range(h * HALF, (h + 1) * HALF):
                            pool.indirect_dma_start(
                                rec_d[s], bass.IndirectOffsetOnAxis(ap=idx[:, k:k + 1], axis=0),
                                rring[:, k, :], None, bounds_check=last,
                                oob_is_err=False).then_inc(d["scat"][h], 16)

                rounds(pool, COLS // RING, step)

            pool.wait_ge(s_zeroed, 16)
            scatter(0, P * SORTS[0].tiles - 1)
            pool.wait_ge(srt[1]["linear"], 64)
            with unsorted(pool):
                scatter(1, E - 1)
            pool.wait_ge(s_rows, 1)
            for l, tab in enumerate((x, h1_d, x1_d)):
                d = lay[l]
                if l:
                    pool.wait_ge(lay[l - 1]["stored_dma"], 16 * NSEPT)
                def step(i):
                    for q in range(4):
                        if due(i * QUART + T0[l]):
                            pool.wait_ge(d["mm"][q], i * QUART + T0[l])
                        pool.wait_ge(d["idx"][q], i + (1 + R0[l]))
                        pool.sem_inc(s_go, 1)
                        for k in range(q * QUART, (q + 1) * QUART):
                            pool.indirect_dma_start(
                                G[:, k, 0:D], None, tab,
                                bass.IndirectOffsetOnAxis(ap=idx[:, k:k + 1], axis=0)).then_inc(d["gath"][q], 16)

                rounds(pool, SORTS[LSORT[l]].tiles // RING, step)
                if l < 2:
                    pool.wait_ge(d["add"][3], T0[l + 1])

                    def step(i):
                        if due(i):
                            pool.wait_ge(d["tr"], i)
                        nc.gpsimd.tensor_copy(mean_st.rearrange("p (b c) -> p b c", c=D), agg[:, bass.ds(i * SEPT, SEPT), 0:D]).then_inc(d["meanst"], 1)

                    rounds(pool, NSEPT, step)

        @block.scalar
        def _(act):
            words = (((raw[:, DST, :], locs[:, 0, :], rawf[:, WT, :], locs[:, 0, :]),
                      (raw[:, SRC, :], raw[:, DST, :], rawf[:, WT1, :], raw[:, ET, :])))

            def deviations(i, d, number):
                act.wait_ge(d["for_root"], i + 1)
                act.sem_inc(s_go_act, 1)
                for j in range(SEPT):
                    nc.scalar.activation(squares[:, j * D:(j + 1) * D], node(H1, i, j), ACT.Square, bias=stats[:, NEG_MEAN, j:j + 1],
                                         accum_out=stats[:, DEVIATION, j:j + 1]).then_inc(d["squares"], 1)
                act.wait_ge(d["squares"], number)
                nc.scalar.activation(stats[:, STD, :], stats[:, DEVIATION, :], ACT.Sqrt, bias=eps_ln[:, 0:1], scale=1.0 / D).then_inc(d["root"], 1)

            def fill(s):
                d = srt[s]

                def step(i):
                    for h in range(2):
                        if due(i * (HALF * 16)):
                            act.wait_ge(d["scat"][h], i * (HALF * 16))
                        for wd, a in enumerate(words[s]):
                            to = (rringf if wd else rring)[:, h * HALF:(h + 1) * HALF, wd]
                            nc.scalar.activation(to, a[:, bass.ds(i * RING + h * HALF, HALF)], ACT.Copy).then_inc(d["rec"], 1)

                rounds(act, COLS // RING, step)

            act.wait_ge(s_sources, 48)
            act.wait_ge(s_edges, N_EDGES)
            act.wait_ge(srt[0]["keys"], 1)
            for wd, a in enumerate(words[1]):
                nc.scalar.activation((natural.bitcast(F32) if wd else natural)[:, :, wd], a, ACT.Copy).then_inc(srt[1]["shaped"], 1)
            fill(0)
            scattered(act, 0)
            with unsorted(act):
                fill(1)
                scattered(act, 1)
            act.wait_ge(s_nodes, N_NODES)
            act.wait_ge(s_wt, 1)
            nc.scalar.activation(WT_sb[:].rearrange("p a b -> p (a b)"), bank(7), ACT.Copy).then_inc(s_wtc, 1)
            for l in range(2):
                d = lay[l]
                if l == 0:
                    act.wait_ge(srt[0]["first"], 16)
                else:
                    for q in range(4):
                        act.wait_ge(lay[0]["gath"][q], SORTS[0].tiles // 4 * 16)
                        act.wait_ge(lay[0]["sel"][q], T0[1])
                def step(i, own):
                    for q in range(4):
                        ks = slice(q * QUART, (q + 1) * QUART)
                        frm = bass.ds(i * RING + q * QUART, QUART)
                        if due(i * (QUART * 16)):
                            act.wait_ge(d["gath"][q], i * (QUART * 16))
                        nc.scalar.activation(idx[:, ks], S[0][:, frm, 0], ACT.Copy).then_inc(d["idx"][q], 1)
                        if due(i * QUART + T0[l]):
                            act.wait_ge(d["sel"][q], i * QUART + T0[l])
                        nc.scalar.activation(rringf[:, ks, 1:3], Sf[0][:, frm, 1:3], ACT.Copy).then_inc(d["rec"][q], 1)

                    if own:
                        if due(i):
                            act.wait_ge(d["ownT"], i)
                        nc.scalar.activation(own_st.rearrange("p (b c) -> p b c", c=D), (X, H1)[l][:, bass.ds(i * SEPT, SEPT), :], ACT.Copy).then_inc(d["ownst"], 1)

                step(0, True)
                act.wait_ge(srt[0]["loaded"], 16)
                with act.Fori(1, NSEPT) as i:
                    step(i, True)
                with act.Fori(NSEPT, ROUNDS[l]) as i:
                    step(i, False)
                def transposed(i):
                    act.wait_ge(d["tr"], i + 1)
                    if due(i):
                        act.wait_ge(d["lin"], i)
                    nc.scalar.activation(meanT, trs(), ACT.Copy).then_inc(d["trc"], 1)

                def step(i, ahead):
                    if ahead:
                        transposed(i + 1)
                    Hi = H1[:, bass.ds(i * SEPT, SEPT), :]
                    act.wait_ge(d["comb"], (i + 1) * SEPT)
                    if l == 0:
                        nc.scalar.activation(Hi, Hi, ACT.Relu).then_inc(d["stored"], 1)
                    else:
                        nc.scalar.activation(Hi, Hi, ACT.Relu).then_inc(d["relu"], 1)
                        act.wait_ge(d["relu"], i + 1)
                        act.sem_inc(s_go_act, 1)
                        for j in range(SEPT):
                            nc.scalar.activation(squares[:, j * D:(j + 1) * D], node(H1, i, j), ACT.Square,
                                                 accum_out=stats[:, SQUARES, j:j + 1]).then_inc(d["squares"], 1)
                        act.wait_ge(d["squares"], i * (2 * SEPT) + SEPT)
                        nc.scalar.activation(stats[:, NORM, :], stats[:, SQUARES, :], ACT.Sqrt).then_inc(d["root"], 1)
                        deviations(i, d, i * (2 * SEPT) + 2 * SEPT)

                transposed(0)
                rounds_ahead(act, NSEPT, step)
            d = lay[2]
            act.wait_ge(srt[1]["local"], 1)
            for q in range(4):
                act.wait_ge(lay[1]["gath"][q], SORTS[0].tiles // 4 * 16)
                act.wait_ge(lay[1]["sel"][q], T0[2])
                act.wait_ge(lay[1]["mm"][q], T0[2])
            def records(i):
                nc.scalar.activation(rringf[:, :, 1:4], Sf[1][:, bass.ds(i * RING, RING), 1:4], ACT.Copy).then_inc(d["rec"][0], 1)

            def indices(i, q):
                nc.scalar.activation(idx[:, q * QUART:(q + 1) * QUART], S[1][:, bass.ds(i * RING + q * QUART, QUART), 0], ACT.Copy).then_inc(d["idx"][q], 1)

            def relations(i):
                act.wait_ge(d["relT"], i + 1)
                nc.scalar.activation(relT.rearrange("p a b -> p (a b)"), bank(0), ACT.Copy).then_inc(d["relTc"], 1)

            def step(i, ahead):
                if ahead:
                    act.wait_ge(d["coefn"], i + 1)
                    records(i + 1)
                for q in range(4):
                    if ahead:
                        act.wait_ge(d["gath"][q], i * (QUART * 16) + QUART * 16)
                        indices(i + 1, q)
                    if q == 2 and ahead:
                        relations(i + 1)
                    if due(i):
                        act.wait_ge(d["w"][q // 2], i)
                    for k in range(0, QUART, 2):
                        t = q * QUART + k
                        act.wait_ge(d["mm"][q], i * QUART + (T0[2] + k + 2))
                        nc.scalar.activation(Ub[:, :, t:t + 2, :].rearrange("p b t j -> p t b j"),
                                             basis_sums(t, 2).rearrange("p (t b j) -> p t b j", t=2, j=DWIN), ACT.Copy).then_inc(d["uc"][q], 1)

            records(0)
            for q in range(4):
                indices(0, q)
            relations(0)
            rounds_ahead(act, ROUNDS[2], step)
            for q in range(4):
                act.wait_ge(d["add"][q], T0[3])
            def relu(i):
                if due(i):
                    act.wait_ge(d["tr"], i)
                nc.scalar.activation(relu2, reprT[:, bass.ds(i * (SEPT * P), SEPT * P)], ACT.Relu, bias=brel_c[:, 0:1]).then_inc(d["nst"], 1)

            def step(i, ahead):
                if ahead:
                    relu(i + 1)
                deviations(i, d, i * SEPT + SEPT)

            relu(0)
            rounds_ahead(act, NSEPT, step)

        @block.tensor
        def _(pe):
            pe.wait_ge(s_const, 3)
            pe.wait_ge(s_ones, 3)
            def opening(s):
                nc.tensor.matmul(bank(s, SORTS[s].cells), onesf[0:1, :], start[0:1, 0:SORTS[s].cells], start=True, stop=True, skip_group_check=True).then_inc(srt[s]["opened"], 1)

            def count(s, rhs, number):
                pe.wait_ge(srt[s]["count_oh"], number)
                nc.tensor.matmul(bank(s, SORTS[s].cells), ones[:], rhs[:, 0:SORTS[s].cells], start=False, stop=True, skip_group_check=True).then_inc(srt[s]["counted"], 1)

            def windows(s):
                st = SORTS[s]
                pe.wait_ge(srt[s]["marks"], 1)
                for c in range(up(st.tiles, 512) // 512):
                    n = min(512, st.tiles - c * 512)
                    for j in range(st.chunks):
                        nc.tensor.matmul(bank(2 + c, n), ones[:], mark[j][:, c * 512:c * 512 + n], start=(j == 0), stop=(j == st.chunks - 1)).then_inc(srt[s]["marked"], 1)

            def rank(s, k, number):
                d, cells = srt[s], SORTS[s].cells
                pe.wait_ge(d["oh"], number)
                nc.tensor.matmul(bank(s, cells), strict[:], oh[:, k, 0:cells], start=False, stop=True, skip_group_check=True).then_inc(d["ranked"], 1)
                pe.wait_ge(d["prod"], number)
                nc.tensor.matmul(bank(s, cells), comp[:], oh[:, k, 0:cells], start=False, stop=True, skip_group_check=True).then_inc(d["summed"], 1)

            pe.wait_ge(srt[0]["blank"], 1)
            opening(0)
            opening(1)

            def count_bin(b, k, reduced):
                pe.wait_ge(srt[0]["count_oh"], b + 1)
                if reduced is not None:
                    pe.wait_ge(srt[0]["reduced"], reduced)
                for c in range(0, COLS, COUNT_COLS):
                    last = nc.tensor.matmul(bank(2 + k, COUNT_COLS), ones[:], equal[:, k, c:c + COUNT_COLS], start=(c == 0), stop=(c + COUNT_COLS == COLS))
                last.then_inc(srt[0]["counted"], 1)

            count_bin(0, 0, None)
            count_bin(1, 1, None)
            with pe.Fori(0, SORTS[0].bins // 2 - 1) as i:
                count_bin(i * 2 + 2, 0, i * 2 + 1)
                count_bin(i * 2 + 3, 1, i * 2 + 2)
            count_bin(SORTS[0].bins - 1, 0, SORTS[0].bins - 2)
            pe.wait_ge(srt[0]["start"], 1)
            opening(0)

            def step(i):
                for h in range(2):
                    rank(0, h, i * 2 + h + 1)
                    for j in range(SORTS[1].per_half):
                        count(1, oh1[:, j % 4, :], (i * 2 + h) * SORTS[1].per_half + j + 1)

            step(0)
            pe.wait_ge(srt[1]["dropped"], 1)
            nc.tensor.matmul(bank(7, 2), onesP[:], drops[:, 0:2], start=True, stop=True).then_inc(srt[1]["dropsum"], 1)
            windows(0)
            with pe.Fori(1, SORTS[0].groups // 2) as i:
                step(i)
            windows(1)
            for c in range(up(SORTS[1].tiles, 512) // 512):
                n = min(512, SORTS[1].tiles - c * 512)
                pe.wait_ge(srt[1]["split"], c + 1)
                for j in range(SORTS[1].chunks):
                    last = nc.tensor.matmul(bank(2 + c, n), pad[:, j, :], mark[j][:, c * 512:c * 512 + n], start=(j == 0), stop=(j == SORTS[1].chunks - 1))
                last.then_inc(srt[1]["marked"], 1)
            pe.wait_ge(srt[1]["start"], 1)
            with unsorted(pe):
                opening(1)

                def step(i):
                    for k in range(2):
                        rank(1, k, i * 2 + k + 1)

                rounds(pe, SORTS[1].groups // 2, step)
            pe.wait_ge(s_small, N_SMALL)
            for j in range(4):
                last = nc.tensor.transpose(bank(7, P, j * P), wtmp[:, j, :], ident[:])
            last.then_inc(s_wt, 1)
            pe.wait_ge(s_wtc, 1)
            pe.wait_ge(s_rows, 1)
            for l in range(2):
                d = lay[l]
                def step(i, own):
                    for q in range(4):
                        pe.wait_ge(d["sel"][q], i * QUART + (QUART + T0[l]))
                        if q > 1:
                            pe.wait_ge(d["add"][q - 2], i * QUART + (QUART + T0[l]))
                        elif due(i * QUART + T0[l]):
                            pe.wait_ge(d["add"][q + 2], i * QUART + T0[l])
                        pe.wait_ge(d["gath"][q], i * (QUART * 16) + QUART * 16)
                        for t in range(q * QUART, (q + 1) * QUART):
                            nc.tensor.matmul(sums(t), sel[:, t, :], G[:, t, :], start=True, stop=True).then_inc(d["mm"][q], 1)
                        if own and q == 1:
                            pe.wait_ge(d["ownst"], i + 1)
                            for j in range(SEPT):
                                last = nc.tensor.transpose(trs(j, 1), own_st[:, j * D:(j + 1) * D], ident[:])
                            last.then_inc(d["ownT"], 1)
                    if own:
                        pe.wait_ge(d["ownTc"], i + 1)
                        if due(i):
                            pe.wait_ge(d["own"], i)
                        for j in range(SEPT):
                            nc.tensor.matmul(lin(j, 1), ownT[:, j * D:(j + 1) * D], WT_sb[:, 2 * l, :], start=True, stop=False)
                            last = nc.tensor.matmul(lin(j, 1), onesf[:], bias[:, l, :], start=False, stop=True)
                        last.then_inc(d["ownlin"], 1)

                step(0, True)
                with pe.Fori(1, NSEPT) as i:
                    step(i, True)
                with pe.Fori(NSEPT, ROUNDS[l]) as i:
                    step(i, False)
                for q in range(4):
                    pe.wait_ge(d["add"][q], T0[l + 1])

                def transposes(i):
                    pe.wait_ge(d["meanst"], i + 1)
                    for j in range(SEPT):
                        last = nc.tensor.transpose(trs(j, 1), mean_st[:, j * D:(j + 1) * D], ident[:])
                    last.then_inc(d["tr"], 1)

                def step(i, ahead):
                    pe.wait_ge(d["trc"], i + 1)
                    if ahead:
                        transposes(i + 1)
                    if due(i):
                        pe.wait_ge(d["comb"], i * SEPT)
                    for j in range(SEPT):
                        last = nc.tensor.matmul(lin(j, 1), meanT[:, j * D:(j + 1) * D], WT_sb[:, 2 * l + 1, :], start=True, stop=True)
                    last.then_inc(d["lin"], 1)

                transposes(0)
                rounds_ahead(pe, NSEPT, step)
                pe.wait_ge(d["stored"], NSEPT * (1, SEPT)[l])
            d = lay[2]
            def relations(i):
                pe.wait_ge(d["rel"], i + 1)
                for q in range(4):
                    last = nc.tensor.matmul(bank(0, P, q * P), rel[:, q * QUART:(q + 1) * QUART, :].rearrange("p a b -> p (a b)"), ident_h[:], start=True, stop=True)
                last.then_inc(d["relT"], 1)

            def coefficients(i):
                pe.wait_ge(d["relTc"], i + 1)
                for q in range(4):
                    last = nc.tensor.matmul(bank(1, 32, q * 32), relT[:, q, :], wcd[:].rearrange("p a b -> p (a b)"), start=True, stop=True)
                last.then_inc(d["coef"], 1)

            def times_bases(i, h):
                for q in (2 * h, 2 * h + 1):
                    pe.wait_ge(d["uc"][q], i * 2 + 2)
                pe.wait_ge(d["add"][2 * h + 1], i * QUART + T0[2])
                for b in range(BASES):
                    last = nc.tensor.matmul(bank(6 + h, HALF * DWIN), Wr[:, b, :], Ub[:, b, h * HALF:(h + 1) * HALF, :].rearrange("p t j -> p (t j)"), start=(b == 0), stop=(b == BASES - 1))
                last.then_inc(d["w"][h], 1)

            def step(i, before, ahead):
                for q in range(4):
                    if q < 2 and before is not None:
                        times_bases(before, q)
                    pe.wait_ge(d["cmat"], i * 4 + (q + 1))
                    if q > 1:
                        pe.wait_ge(d["uc"][q - 2], i * 2 + 2)
                    elif before is not None:
                        pe.wait_ge(d["uc"][q + 2], before * 2 + 2)
                    pe.wait_ge(d["gath"][q], i * (QUART * 16) + QUART * 16)
                    for t in range(q * QUART, (q + 1) * QUART):
                        nc.tensor.matmul(basis_sums(t), G[:, t, 0:D],
                                         C[:, t, :, :].rearrange("p b j -> p (b j)"), start=True, stop=True).then_inc(d["mm"][q], 1)
                    if q == 1 and ahead:
                        relations(i + 1)
                if ahead:
                    coefficients(i + 1)

            relations(0)
            coefficients(0)
            rounds_behind(pe, ROUNDS[2], step)
            for h in range(2):
                times_bases(ROUNDS[2] - 1, h)

            def step(i):
                pe.wait_ge(d["nst"], i + 1)
                if due(i):
                    pe.wait_ge(d["relu"], i * 2)
                for j in range(SEPT):
                    last = nc.tensor.transpose(trs(j, 1), relu2[:, j * P:(j + 1) * P], ident[:])
                last.then_inc(d["tr"], 1)

            rounds(pe, NSEPT, step)

        @block.vector
        def _(dve):
            n_chain = [0]

            def link(ins):
                n_chain[0] += 1
                ins.then_inc(s_dve, 1)
                dve.wait_ge(s_dve, n_chain[0])

            def row_sums(i):
                dve.sem_inc(s_go_dve, 1)
                return nc.vector.tensor_reduce(stats[:, SUM, :], H1[:, bass.ds(i * SEPT, SEPT), :], AX, ALU.add)

            def means(d):
                nc.vector.tensor_scalar(stats[:, NEG_MEAN, :], stats[:, SUM, :], -1.0 / D, None, ALU.mult).then_inc(d["for_root"], 1)

            def normalized(nlink, d, i, root):
                dve.wait_ge(d["root"], root)
                nlink(nc.vector.reciprocal(stats[:, STD, :], stats[:, STD, :]))
                for j in range(SEPT):
                    nc.vector.tensor_scalar(node(X, i, j), node(H1, i, j), stats[:, NEG_MEAN, j:j + 1], stats[:, STD, j:j + 1], ALU.add, ALU.mult).then_inc(d["stored"], 1)
                dve.wait_ge(d["stored"], i * SEPT + SEPT)

            nc.vector.memset(eps_ln[:], EPS_LN).then_inc(s_ones, 1)
            nc.vector.memset(ones[:], 1.0).then_inc(s_ones, 1)
            nc.vector.memset(onesP[:], 1.0).then_inc(s_ones, 1)
            link(nc.vector.memset(keys[:, :, COLS:], 0.0))
            dve.wait_ge(s_iota, 2)
            link(nc.vector.tensor_copy(iota_b[:], iota_i[:]))
            link(nc.vector.tensor_copy(iota_f[:], iota_i[:, 0:P]))
            dve.wait_ge(s_const, 3)
            link(nc.vector.tensor_copy(ident_h[:], ident[:]))
            dve.wait_ge(s_sources, 48)

            def cells(s, t):
                return t[:, 0:SORTS[s].cells].rearrange("p (l b) -> p l b", b=SORTS[s].wide)

            def onehot(s, to, g):
                B, L = SORTS[s].wide, SORTS[s].lanes
                return nc.vector.tensor_tensor(
                    cells(s, to), iota_b[:, 0:B].unsqueeze(1).to_broadcast([P, L, B]),
                    keys[:, s, bass.ds(g * L, L)].unsqueeze(2).to_broadcast([P, L, B]), ALU.is_equal)

            def windows_of_edges(s):
                st, edge_node = SORTS[s], raw[:, (SRC, DST)[s], :]
                link(nc.vector.tensor_scalar(kt, edge_node, st.shift, None, ALU.logical_shift_right))
                link(nc.vector.tensor_copy(keys[:, s, 0:COLS], kt))
                if s == 0:
                    link(nc.vector.tensor_scalar(kl, edge_node, st.window - 1, None, ALU.bitwise_and))
                    nc.vector.tensor_copy(locs[:, s, :], kl).then_inc(srt[s]["keys"], 1)
                    dve.wait_ge(srt[s]["keys"], 1)

            def starts(s):
                st, d, L = SORTS[s], srt[s], SORTS[s].lanes
                tiles, incl, ones_r, first = (tot[:, j, 0:st.bins] for j in range(4))
                if s:
                    link(nc.vector.tensor_copy(prod[:, 0:st.cells], bank(s, st.cells)))
                counts = cells(s, prod)
                link(nc.vector.tensor_reduce(first, counts.rearrange("p l b -> p b l")[:, 0:st.bins, :], AX, ALU.add))
                link(nc.vector.tensor_scalar(toti[:, 0:st.bins], first, float(P - 1), None, ALU.add))
                link(nc.vector.tensor_scalar(toti[:, 0:st.bins], toti[:, 0:st.bins], 7, None, ALU.logical_shift_right))
                link(nc.vector.tensor_copy(tiles, toti[:, 0:st.bins]))
                link(nc.vector.memset(ones_r, 1.0))
                sl = cells(s, start)
                if s:
                    link(nc.vector.tensor_tensor_scan(incl, ones_r, first, 0.0, ALU.mult, ALU.add))
                    link(nc.vector.tensor_tensor(sl[:, 0, 0:st.bins], incl, first, ALU.subtract))
                    link(nc.vector.scalar_tensor_tensor(first, tiles, float(P), first, ALU.mult, ALU.subtract))
                    for j in range(st.chunks):
                        nb = min(P, st.bins - j * P)
                        link(nc.vector.memset(scratch[:, 0:P], 0.0))
                        link(nc.vector.tensor_copy(scratch[:, 0:nb], first[:, j * P:j * P + nb]))
                        link(nc.vector.tensor_tensor(scratch[:, P:2 * P], scratch[:, 0:P], ident[:], ALU.mult))
                        link(nc.vector.tensor_reduce(col[:, j:j + 1], scratch[:, P:2 * P], AX, ALU.add))
                        link(nc.vector.tensor_copy(pad[:, j, :], col[:, j:j + 1].to_broadcast([P, P])))
                link(nc.vector.tensor_tensor_scan(incl, ones_r, tiles, 0.0, ALU.mult, ALU.add))
                if s == 0:
                    link(nc.vector.tensor_tensor(first, incl, tiles, ALU.subtract))
                    link(nc.vector.tensor_scalar(sl[:, 0, 0:st.bins], first, float(P), None, ALU.mult))
                link(nc.vector.memset(sl[:, :, st.bins:], TRASH))
                for j in range(1, L):
                    link(nc.vector.tensor_tensor(sl[:, j, 0:st.bins], sl[:, j - 1, 0:st.bins], counts[:, j - 1, 0:st.bins], ALU.add))
                dve.sem_inc(d["start"], 1)

            def tables(s):
                st, d = SORTS[s], srt[s]
                incl = tot[:, 1, 0:st.bins]
                for j in range(st.chunks):
                    nb = min(P, st.bins - 1 - j * P)
                    link(nc.vector.memset(prod[:, 0:P], 1e9))
                    link(nc.vector.tensor_copy(prod[:, 0:nb], incl[:, j * P:j * P + nb]))
                    link(nc.vector.tensor_tensor(prod[:, P:2 * P], prod[:, 0:P], ident[:], ALU.mult))
                    link(nc.vector.tensor_reduce(col[:, j:j + 1], prod[:, P:2 * P], AX, ALU.add))
                    link(nc.vector.tensor_scalar(mark[j][:, 0:st.tiles], tiota[:, 0:st.tiles], col[:, j:j + 1], None, ALU.is_ge))
                dve.sem_inc(d["marks"], 1)
                for c in range(up(st.tiles, 512) // 512):
                    n = min(512, st.tiles - c * 512)
                    dve.wait_ge(d["marked"], st.chunks * (c + 1))
                    link(nc.vector.tensor_copy(table[32 * s:32 * s + 1, c * 512:c * 512 + n], PS[0:1, (2 + c) * 512:(2 + c) * 512 + n]))
                    if s:
                        nc.vector.tensor_copy(wrow[:, c * 512:c * 512 + n], bank(2 + c, n)).then_inc(d["split"], 1)
                if s:
                    chunks = up(st.tiles, 512) // 512
                    for c in range(chunks):
                        n = min(512, st.tiles - c * 512)
                        dve.wait_ge(d["marked"], st.chunks * chunks + c + 1)
                        link(nc.vector.scalar_tensor_tensor(table[64:65, c * 512:c * 512 + n], tiota[64:65, c * 512:c * 512 + n], float(P),
                                                            PS[64:65, (2 + c) * 512:(2 + c) * 512 + n], ALU.mult, ALU.subtract))
                    dve.sem_inc(d["offsets"], 1)

            def ranking(s, beside, between):
                st, d, L = SORTS[s], srt[s], SORTS[s].lanes
                acc, per = bank(s, st.cells), st.per_half
                dve.wait_ge(d["opened"], 2)
                onehot(s, oh[:, 0, :], 0).then_inc(d["oh"], 1)

                def step(i):
                    for h in range(2):
                        for j in range(per):
                            g = h * per + j
                            if due(i * (2 * per) + g):
                                dve.wait_ge(d["summed"], i * (2 * per) + g)
                            onehot(s, oh[:, (g + 1) % 2, :], i * (2 * per) + g + 1).then_inc(d["oh"], 1)
                            if due(i * (2 * per) + g):
                                dve.wait_ge(d["pos"], i * (2 * per) + g)
                            dve.wait_ge(d["ranked"], i * (2 * per) + g + 1)
                            nc.vector.tensor_tensor(prod[:, 0:st.cells], acc, oh[:, g % 2, 0:st.cells], ALU.mult).then_inc(d["prod"], 1)
                            beside(i, g)
                            dve.wait_ge(d["prod"], i * (2 * per) + g + 1)
                            with nc.allow_low_precision(reason="whole numbers, exact in float32"):
                                nc.vector.tensor_reduce(posi[:, 0, j * L:(j + 1) * L], cells(s, prod), AX, ALU.add).then_inc(d["pos"], 1)
                        dve.wait_ge(d["pos"], i * (2 * per) + (h + 1) * per)
                        here = idx[:, h * HALF:(h + 1) * HALF]
                        if s == 0:
                            nc.vector.tensor_scalar(posi[:, 1, :], posi[:, 0, :], P - 1, None, ALU.bitwise_and).then_inc(d["split"], 1)
                            nc.vector.tensor_scalar(posi[:, 2, :], posi[:, 0, :], 7, None, ALU.logical_shift_right).then_inc(d["split"], 1)
                            dve.wait_ge(d["split"], i * 4 + h * 2 + 2)
                        if due(i * (HALF * 16)):
                            dve.wait_ge(d["scat"][h], i * (HALF * 16))
                        if s == 0:
                            nc.vector.scalar_tensor_tensor(here, posi[:, 1, :], float(st.tiles), posi[:, 2, :], ALU.mult, ALU.add).then_inc(d["idx"], 1)
                        else:
                            nc.vector.tensor_copy(here, posi[:, 0, :]).then_inc(d["idx"], 1)
                            dve.wait_ge(d["idx"], i * 2 + h + 1)

                step(0)
                between()
                with dve.Fori(1, COLS // RING) as i:
                    step(i)
                dve.wait_ge(d["summed"], st.groups)
                dve.wait_ge(d["oh"], st.groups + 1)

            windows_of_edges(0)
            nc.vector.memset(start[:], 0.0).then_inc(srt[0]["blank"], 1)
            dve.wait_ge(srt[0]["opened"], 1)

            def mark_bin(b, k, counted):
                if counted is not None:
                    dve.wait_ge(srt[0]["counted"], counted)
                nc.vector.tensor_scalar(equal[:, k, :], keys[:, 0, 0:COLS], iota_f[:, bass.ds(b, 1)], None, ALU.is_equal).then_inc(srt[0]["count_oh"], 1)

            def reduce_bin(b, k):
                dve.wait_ge(srt[0]["counted"], b + 1)
                dve.sem_inc(s_go_dve, 1)
                nc.vector.tensor_reduce(cells(0, prod)[:, :, bass.ds(b, 1)].rearrange("p l a -> p (l a)"),
                                        bank(2 + k, COUNT_COLS).rearrange("p (g l) -> p l g", l=SORTS[0].lanes), AX, ALU.add).then_inc(srt[0]["reduced"], 1)

            mark_bin(0, 0, None)
            mark_bin(1, 1, None)
            reduce_bin(0, 0)
            with dve.Fori(0, SORTS[0].bins // 2 - 1) as i:
                mark_bin(i * 2 + 2, 0, i * 2 + 1)
                reduce_bin(i * 2 + 1, 1)
                mark_bin(i * 2 + 3, 1, i * 2 + 2)
                reduce_bin(i * 2 + 2, 0)
            mark_bin(SORTS[0].bins - 1, 0, SORTS[0].bins - 2)
            reduce_bin(SORTS[0].bins - 2, 1)
            reduce_bin(SORTS[0].bins - 1, 0)
            dve.wait_ge(srt[0]["reduced"], SORTS[0].bins)
            dve.wait_ge(srt[1]["opened"], 1)
            starts(0)
            dve.wait_ge(s_edges, N_EDGES)
            windows_of_edges(1)
            def order_and_tables():
                link(nc.vector.tensor_tensor(locs[:, 1, 0:COLS - 1], keys[:, 1, 0:COLS - 1], keys[:, 1, 1:COLS], ALU.is_gt))
                link(nc.vector.tensor_reduce(drops[:, 0:1], locs[:, 1, 0:COLS - 1], AX, ALU.add))
                link(nc.vector.tensor_scalar(after[:], after[:], SORTS[1].shift, None, ALU.logical_shift_right))
                link(nc.vector.tensor_copy(drops[:, 2:3], after[:]))
                link(nc.vector.tensor_copy(drops[:, 3:4], keys[:, 1, COLS - 1:COLS]))
                link(nc.vector.tensor_tensor(drops[:, 1:2], drops[:, 3:4], drops[:, 2:3], ALU.is_gt))
                dve.sem_inc(srt[1]["dropped"], 1)
                tables(0)

            def counts_of_second(i, g):
                per = SORTS[1].per_half
                for j in range(per):
                    if j == 0 and due(i * (2 * per) + g * per):
                        dve.wait_ge(srt[1]["counted"], i * (2 * per) + g * per)
                    onehot(1, oh1[:, j % 4, :], i * (2 * per) + (g * per + j)).then_inc(srt[1]["count_oh"], 1)

            ranking(0, counts_of_second, order_and_tables)
            dve.wait_ge(srt[1]["dropsum"], 1)
            link(nc.vector.tensor_reduce(drops[:, 2:3], bank(7, 2), AX, ALU.add))
            nc.vector.tensor_copy(flag[:], drops[0:1, 2:3]).then_inc(srt[1]["flag"], 1)
            dve.wait_ge(srt[1]["counted"], SORTS[1].groups)
            starts(1)
            tables(1)
            with unsorted(dve):
                scattered(dve, 0)
                ranking(1, lambda i, g: None, lambda: None)
                scattered(dve, 1)

            def bc(t):
                return t.unsqueeze(2).to_broadcast([P, SEPT, D])

            dve.wait_ge(s_preset, 4)
            scattered(dve, 0)
            nc.vector.memset(G[:, :, D:D + 1], 1.0).then_inc(s_rows, 1)
            for l in range(2):
                d = lay[l]
                if l:
                    dve.wait_ge(lay[0]["tr"], NSEPT)
                    dve.wait_ge(lay[0]["stored_dma"], 16 * NSEPT)
                link(nc.vector.memset(agg, 0.0))
                def selections(i, q):
                    dve.wait_ge(d["rec"][q], i + (1 + R0[l]))
                    if due(i * QUART + T0[l]):
                        dve.wait_ge(d["mm"][q], i * QUART + T0[l])
                    for t in range(q * QUART, (q + 1) * QUART):
                        nc.vector.tensor_scalar(sel[:, t, :], iota_f[:], rringf[:, t, 1:2], rringf[:, t, 2:3], ALU.is_equal, ALU.mult).then_inc(d["sel"][q], 1)

                def own_transposed(i):
                    dve.wait_ge(d["ownT"], i + 1)
                    nc.vector.tensor_copy(ownT, trs()).then_inc(d["ownTc"], 1)

                def own_half(i):
                    dve.wait_ge(d["ownlin"], i + 1)
                    nc.vector.tensor_copy(H1[:, bass.ds(i * SEPT, SEPT), :], lin().rearrange("p (b c) -> p b c", c=D)).then_inc(d["own"], 1)

                def step(i, ahead, own):
                    blocks = registers(mybir.EngineType.DVE, 0, i, NBLK - 1)
                    for q in range(4):
                        if q < 3:
                            selections(i, q + 1)
                        elif ahead:
                            selections(i + 1, 0)
                        for k in range(QUART):
                            t = q * QUART + k
                            a = agg[:, bass.ds(blocks[t], 1), :].rearrange("p a c -> p (a c)")
                            dve.wait_ge(d["mm"][q], i * QUART + (T0[l] + k // 2 * 2 + 2))
                            if k:
                                if due(i * QUART + (T0[l] + k)):
                                    dve.wait_ge(d["add"][q], i * QUART + (T0[l] + k))
                            elif q:
                                dve.wait_ge(d["add"][q - 1], i * QUART + (T0[l] + QUART))
                            else:
                                if due(i * QUART + T0[l]):
                                    dve.wait_ge(d["add"][3], i * QUART + T0[l])
                            nc.vector.tensor_tensor(a, a, sums(t), ALU.add).then_inc(d["add"][q], 1)
                        if own and q == 0 and own != "first":
                            own_half(i + -1)
                        if own and q == 2:
                            own_transposed(i)

                selections(0, 0)
                step(0, True, "first")
                with dve.Fori(0, NSEPT - 1) as i:
                    step(i + 1, True, "later")
                own_half(NSEPT - 1)
                with dve.Fori(NSEPT, ROUNDS[l] - 1) as i:
                    step(i, True, None)
                step(ROUNDS[l] - 1, False, None)
                dve.wait_ge(d["add"][3], T0[l + 1])
                if l == 0:
                    link(nc.vector.tensor_scalar(rw[:], agg[:, :, D], EPS_WSUM, None, ALU.max))
                    link(nc.vector.reciprocal(rw[:], rw[:]))

                def combined(i):
                    dve.wait_ge(d["lin"], i + 1)
                    for j in range(SEPT):
                        nc.vector.scalar_tensor_tensor(node(H1, i, j), lin(j, 1), rw[:, bass.ds(i * SEPT + j, 1)], node(H1, i, j), ALU.mult, ALU.add).then_inc(d["comb"], 1)

                def step(i, ahead):
                    n = [0]

                    def nlink(ins):
                        n[0] += 1
                        ins.then_inc(d["nchain"], 1)
                        dve.wait_ge(d["nchain"], i * 4 + n[0])

                    dve.wait_ge(d["root"], i * 2 + 1)
                    nlink(nc.vector.tensor_scalar(stats[:, INV_NORM, :], stats[:, NORM, :], EPS_NORM, None, ALU.max))
                    nlink(nc.vector.reciprocal(stats[:, INV_NORM, :], stats[:, INV_NORM, :]))
                    for j in range(SEPT):
                        nc.vector.scalar_tensor_tensor(node(H1, i, j), node(H1, i, j), stats[:, INV_NORM, j:j + 1], node(X, i, j), ALU.mult, ALU.add).then_inc(d["res"], 1)
                    dve.wait_ge(d["res"], i * SEPT + SEPT)
                    nlink(row_sums(i))
                    means(d)
                    if ahead:
                        combined(i + 1)
                    normalized(nlink, d, i, i * 2 + 2)

                if l == 0:
                    rounds(dve, NSEPT, combined)
                else:
                    combined(0)
                    rounds_ahead(dve, NSEPT, step)
            d = lay[2]
            dve.wait_ge(lay[1]["tr"], NSEPT)
            dve.wait_ge(srt[1]["loaded"], 16 * SORTS[1].tiles)
            nc.vector.scalar_tensor_tensor(Sf[1][:, :, 1], wrow[:], -float(DWIN), Sf[1][:, :, 1], ALU.mult, ALU.add).then_inc(srt[1]["local"], 1)
            link(nc.vector.memset(reprT, 0.0))
            def spread(t, n):
                return t.unsqueeze(2).to_broadcast([P, RING, n])

            def numbers(n):
                return iota_f[:, 0:n].unsqueeze(1).to_broadcast([P, RING, n])

            def relations(i):
                dve.wait_ge(d["rec"][0], i + (1 + R0[2]))
                nc.vector.tensor_tensor(rel, numbers(RELS), spread(rringf[:, :, 3], RELS), ALU.is_equal).then_inc(d["rel"], 1)

            def coefficients(i):
                if due(i * 4):
                    dve.wait_ge(d["cmat"], i * 4)
                nc.vector.tensor_tensor(place, numbers(DWIN), spread(rringf[:, :, 1], DWIN), ALU.is_equal).then_inc(d["node"], 1)
                dve.wait_ge(d["coef"], i + 1)
                nc.vector.tensor_tensor(cn, bank(1, P).rearrange("p (t b) -> p t b", b=BASES),
                                        spread(rringf[:, :, 2], BASES), ALU.mult).then_inc(d["coefn"], 1)

            def matrix(i, q):
                ks = slice(q * QUART, (q + 1) * QUART)
                dve.wait_ge(d["node"], i + 1)
                dve.wait_ge(d["coefn"], i + 1)
                dve.wait_ge(d["mm"][q], i * QUART + T0[2])
                nc.vector.tensor_tensor(C[:, ks, :, :], cn[:, ks, :].unsqueeze(3).to_broadcast([P, QUART, BASES, DWIN]),
                                        place[:, ks, :].unsqueeze(2).to_broadcast([P, QUART, BASES, DWIN]), ALU.mult).then_inc(d["cmat"], 1)

            def additions(i):
                wins = registers(mybir.EngineType.DVE, 32, i, SORTS[1].bins - 1)
                for t in range(RING):
                    q, k = divmod(t, QUART)
                    if t % HALF == 0:
                        dve.wait_ge(d["w"][t // HALF], i + 1)
                    a = reprT[:, bass.ds(wins[t] * DWIN, DWIN)]
                    if t == 0:
                        dve.wait_ge(d["add"][3], i * QUART + T0[2])
                    elif k:
                        dve.wait_ge(d["add"][q], i * QUART + (T0[2] + k))
                    else:
                        dve.wait_ge(d["add"][q - 1], i * QUART + (T0[2] + QUART))
                    nc.vector.tensor_tensor(a, a, bank(6 + t // HALF, DWIN, t % HALF * DWIN), ALU.add).then_inc(d["add"][q], 1)

            def step(i, before, ahead):
                coefficients(i)
                for q in range(4):
                    matrix(i, q)
                if ahead:
                    relations(i + 1)
                if before is not None:
                    additions(before)

            relations(0)
            rounds_behind(dve, ROUNDS[2], step)
            additions(ROUNDS[2] - 1)

            def joined(i):
                dve.wait_ge(d["tr"], i + 1)
                nc.vector.tensor_tensor(H1[:, bass.ds(i * SEPT, SEPT), :], trs().rearrange("p (b c) -> p b c", c=D),
                                        X[:, bass.ds(i * SEPT, SEPT), :], ALU.add).then_inc(d["relu"], 1)
                dve.wait_ge(d["relu"], i * 2 + 1)
                row_sums(i).then_inc(d["relu"], 1)
                dve.wait_ge(d["relu"], i * 2 + 2)

            def step(i, ahead):
                def nlink(ins):
                    ins.then_inc(d["nchain"], 1)
                    dve.wait_ge(d["nchain"], i + 1)

                means(d)
                if ahead:
                    joined(i + 1)
                normalized(nlink, d, i, i + 1)

            joined(0)
            rounds_ahead(dve, NSEPT, step)


_INS = ["x", "src", "dst", "edge_type_32", "edge_weight", "edge_weight1", "L0_gnn_W1", "L0_gnn_b1",
        "L0_gnn_W2", "L0_gnn_b2", "L1_gnn_weight", "L1_gnn_w_comp", "L1_gnn_bias_param"]


def kernel(**inputs):
    import concourse.bacc as bacc
    from concourse.bass_utils import run_bass_kernel_spmd

    nc = bacc.Bacc("TRN2", target_bir_lowering=False, num_devices=1)
    arrays, args = {}, []
    for name in _INS:
        a = np.ascontiguousarray(inputs[name])
        if name == "edge_weight1":
            a = a.reshape(-1)
        arrays[f"in_{name}"] = a
        args.append(nc.dram_tensor(f"in_{name}", a.shape, mybir.dt.from_np(a.dtype), kind="ExternalInput").ap())
    args.append(nc.dram_tensor("out_0", (N, D), F32, kind="ExternalOutput").ap())
    build(nc, *args)
    return run_bass_kernel_spmd(nc, [arrays], core_ids=[0]).results[0]["out_0"]
```
